# Optimizing a Trainium2 kernel written in Bass

```python
import numpy as np
import jax
import jax.numpy as jnp

def _softmax(x, axis=-1):
    return jax.nn.softmax(x, axis=axis)

def _gelu(x):
    return jax.nn.gelu(x, approximate=True)

def _silu(x):
    return jax.nn.silu(x)

def _sigmoid(x):
    return jax.nn.sigmoid(x)

def _layernorm(x, axis=-1, eps=1e-05):
    m = jnp.mean(x, axis=axis, keepdims=True)
    v = jnp.var(x, axis=axis, keepdims=True)
    return (x - m) / jnp.sqrt(v + eps)

def _scatter_add(tgt, idx, src, axis=0):
    return tgt.at[idx].add(src)

def _segment_sum(src, seg, n):
    return jax.ops.segment_sum(src, seg, n)
kernel_name = 'mk_seq_postln_d2_jaxref_r8_1ee4e5'

def setup_inputs(seed: int=0):
    np.random.seed(seed)
    _w = jnp.asarray

    def _L0_attn_setup():
        import jax, jax.numpy as jnp
        import numpy as np
        B, S, D, H = (8, 512, 128, 128)

        def log_g(x):
            return jnp.where(x >= 0, jnp.log(jax.nn.relu(x) + 0.5), -jax.nn.softplus(-x))

        def mingru_layer(inp, W, b):
            gh = jnp.einsum('bsd,ed->bse', inp, W) + b
            gate, hidden = jnp.split(gh, 2, axis=2)
            log_z = -jax.nn.softplus(-gate)
            log_coeffs = -jax.nn.softplus(gate)
            h0_log = jnp.full((inp.shape[0], 1, gate.shape[2]), jnp.log(0.5), inp.dtype)
            log_values = jnp.concatenate([h0_log, log_z + log_g(hidden)], axis=1)
            a_star = jnp.pad(jnp.cumsum(log_coeffs, axis=1), ((0, 0), (1, 0), (0, 0)))
            log_h = a_star + jax.lax.cumlogsumexp(log_values - a_star, axis=1)
            return jnp.exp(log_h)[:, 1:]
        key = jax.random.key(seed)
        k = jax.random.split(key, 5)
        s = 1.0 / np.sqrt(D)
        return {'x': jax.random.normal(k[0], (B, S, D), jnp.float32), 'W0': jax.random.uniform(k[1], (2 * H, D), jnp.float32, -s, s), 'b0': jax.random.uniform(k[2], (2 * H,), jnp.float32, -s, s), 'W1': jax.random.uniform(k[3], (2 * H, H), jnp.float32, -s, s), 'b1': jax.random.uniform(k[4], (2 * H,), jnp.float32, -s, s)}
    _L0_attn_in = _L0_attn_setup()

    def _L0_ffn_setup():
        import jax, jax.numpy as jnp
        import numpy as np
        TOP_K = 2
        key = jax.random.key(seed)
        k0, k1, k2, k3, k4 = jax.random.split(key, 5)
        B, S, H, I, E = (1, 512, 128, 256, 8)
        hidden_states = jax.random.normal(k0, (B, S, H), dtype=jnp.float32)
        wg = jax.random.normal(k1, (E, H), dtype=jnp.float32) * 0.02
        w1 = jax.random.normal(k2, (E, I, H), dtype=jnp.float32) * 0.02
        w3 = jax.random.normal(k3, (E, I, H), dtype=jnp.float32) * 0.02
        w2 = jax.random.normal(k4, (E, H, I), dtype=jnp.float32) * 0.02
        return {'hidden_states': hidden_states, 'wg': wg, 'w1': w1, 'w3': w3, 'w2': w2}
    _L0_ffn_in = _L0_ffn_setup()

    def _L1_attn_setup():
        import jax, jax.numpy as jnp
        import numpy as np
        H, KV, D = (8, 2, 32)
        RD = D // 4
        ROPE_THETA = 10000.0

        def _rope_cos_sin(seq_len, dtype):
            inv_freq = 1.0 / ROPE_THETA ** (jnp.arange(0, RD, 2, dtype=jnp.float32) / RD)
            pos = jnp.arange(seq_len, dtype=jnp.float32)
            freqs = pos[:, None] * inv_freq[None, :]
            emb = jnp.concatenate([freqs, freqs], axis=-1)
            return (jnp.cos(emb).astype(dtype), jnp.sin(emb).astype(dtype))

        def _apply_partial_rope(x, cos, sin):
            x_rot, x_pass = (x[..., :RD], x[..., RD:])
            half = RD // 2
            rot = jnp.concatenate([-x_rot[..., half:], x_rot[..., :half]], axis=-1)
            x_rot = x_rot * cos[None, None] + rot * sin[None, None]
            return jnp.concatenate([x_rot, x_pass], axis=-1)
        key = jax.random.key(seed)
        ks = jax.random.split(key, 5)
        B, S, hid = (4, 256, 128)
        s = 0.02
        return {'hidden_states': jax.random.normal(ks[0], (B, S, hid), jnp.float32), 'Wq': jax.random.normal(ks[1], (hid, H * D * 2), jnp.float32) * s, 'Wk': jax.random.normal(ks[2], (hid, KV * D), jnp.float32) * s, 'Wv': jax.random.normal(ks[3], (hid, KV * D), jnp.float32) * s, 'Wo': jax.random.normal(ks[4], (H * D, hid), jnp.float32) * s}
    _L1_attn_in = _L1_attn_setup()

    def _L1_ffn_setup():
        import jax, jax.numpy as jnp
        import numpy as np
        B, S, D, H, O, E, K = (4, 256, 128, 256, 128, 8, 2)
        key = jax.random.key(seed)
        ks = jax.random.split(key, 8)
        x = jax.random.normal(ks[0], (B, S, D), dtype=jnp.float32)
        gate_w = jax.random.uniform(ks[1], (E, D), dtype=jnp.float32, minval=-1, maxval=1) * np.sqrt(6.0 / D)
        gate_b = jnp.zeros((E,), dtype=jnp.float32)
        w1 = jax.random.uniform(ks[2], (E, D, H), dtype=jnp.float32, minval=-1, maxval=1) * np.sqrt(6.0 / D)
        b1 = jnp.zeros((E, H), dtype=jnp.float32)
        w2 = jax.random.uniform(ks[3], (E, H, O), dtype=jnp.float32, minval=-1, maxval=1) * np.sqrt(6.0 / H)
        b2 = jnp.zeros((E, O), dtype=jnp.float32)
        return {'x': x, 'gate_w': gate_w, 'gate_b': gate_b, 'w1': w1, 'b1': b1, 'w2': w2, 'b2': b2}
    _L1_ffn_in = _L1_ffn_setup()
    _d = {'L0_attn_x': _L0_attn_in['x'], 'L0_attn_W0': _L0_attn_in['W0'], 'L0_attn_b0': _L0_attn_in['b0'], 'L0_attn_W1': _L0_attn_in['W1'], 'L0_attn_b1': _L0_attn_in['b1'], 'L0_ffn_wg': _L0_ffn_in['wg'], 'L0_ffn_w1': _L0_ffn_in['w1'], 'L0_ffn_w3': _L0_ffn_in['w3'], 'L0_ffn_w2': _L0_ffn_in['w2'], 'L1_attn_Wq': _L1_attn_in['Wq'], 'L1_attn_Wk': _L1_attn_in['Wk'], 'L1_attn_Wv': _L1_attn_in['Wv'], 'L1_attn_Wo': _L1_attn_in['Wo'], 'L1_ffn_gate_w': _L1_ffn_in['gate_w'], 'L1_ffn_gate_b': _L1_ffn_in['gate_b'], 'L1_ffn_w1': _L1_ffn_in['w1'], 'L1_ffn_b1': _L1_ffn_in['b1'], 'L1_ffn_w2': _L1_ffn_in['w2'], 'L1_ffn_b2': _L1_ffn_in['b2']}
    _x0 = _d['L0_attn_x']
    _d['L0_attn_x'] = jax.random.normal(jax.random.fold_in(jax.random.key(seed), 1), (4, 1024, 128), dtype=_x0.dtype)
    del _x0
    return _d

def reference(L0_attn_x, L0_attn_W0, L0_attn_b0, L0_attn_W1, L0_attn_b1, L0_ffn_wg, L0_ffn_w1, L0_ffn_w3, L0_ffn_w2, L1_attn_Wq, L1_attn_Wk, L1_attn_Wv, L1_attn_Wo, L1_ffn_gate_w, L1_ffn_gate_b, L1_ffn_w1, L1_ffn_b1, L1_ffn_w2, L1_ffn_b2):

    def _L0_attn_ref(x, W0, b0, W1, b1):
        import jax, jax.numpy as jnp
        import numpy as np
        B, S, D, H = (8, 512, 128, 128)

        def log_g(x):
            return jnp.where(x >= 0, jnp.log(jax.nn.relu(x) + 0.5), -jax.nn.softplus(-x))

        def mingru_layer(inp, W, b):
            gh = jnp.einsum('bsd,ed->bse', inp, W) + b
            gate, hidden = jnp.split(gh, 2, axis=2)
            log_z = -jax.nn.softplus(-gate)
            log_coeffs = -jax.nn.softplus(gate)
            h0_log = jnp.full((inp.shape[0], 1, gate.shape[2]), jnp.log(0.5), inp.dtype)
            log_values = jnp.concatenate([h0_log, log_z + log_g(hidden)], axis=1)
            a_star = jnp.pad(jnp.cumsum(log_coeffs, axis=1), ((0, 0), (1, 0), (0, 0)))
            log_h = a_star + jax.lax.cumlogsumexp(log_values - a_star, axis=1)
            return jnp.exp(log_h)[:, 1:]
        h1 = mingru_layer(x, W0, b0)
        out = mingru_layer(h1, W1, b1)
        return out

    def _L0_ffn_ref(hidden_states, wg, w1, w3, w2):
        import jax, jax.numpy as jnp
        import numpy as np
        TOP_K = 2
        orig_shape = hidden_states.shape
        H = orig_shape[-1]
        E = wg.shape[0]
        x = hidden_states.reshape(-1, H)
        router_logits = x @ wg.T
        probs = jax.nn.softmax(router_logits, axis=-1)
        topk_w, topk_idx = jax.lax.top_k(probs, TOP_K)
        topk_w = topk_w / jnp.sum(topk_w, axis=-1, keepdims=True)
        expert_w = jnp.sum(jax.nn.one_hot(topk_idx, E, dtype=x.dtype) * topk_w[..., None], axis=1)
        h1 = jnp.einsum('th,eih->tei', x, w1)
        h3 = jnp.einsum('th,eih->tei', x, w3)
        y = jnp.einsum('tei,ehi->teh', jax.nn.silu(h1) * h3, w2)
        out = jnp.einsum('te,teh->th', expert_w, y)
        return out.reshape(orig_shape)

    def _L1_attn_ref(hidden_states, Wq, Wk, Wv, Wo):
        import jax, jax.numpy as jnp
        import numpy as np
        H, KV, D = (8, 2, 32)
        RD = D // 4
        ROPE_THETA = 10000.0

        def _rope_cos_sin(seq_len, dtype):
            inv_freq = 1.0 / ROPE_THETA ** (jnp.arange(0, RD, 2, dtype=jnp.float32) / RD)
            pos = jnp.arange(seq_len, dtype=jnp.float32)
            freqs = pos[:, None] * inv_freq[None, :]
            emb = jnp.concatenate([freqs, freqs], axis=-1)
            return (jnp.cos(emb).astype(dtype), jnp.sin(emb).astype(dtype))

        def _apply_partial_rope(x, cos, sin):
            x_rot, x_pass = (x[..., :RD], x[..., RD:])
            half = RD // 2
            rot = jnp.concatenate([-x_rot[..., half:], x_rot[..., :half]], axis=-1)
            x_rot = x_rot * cos[None, None] + rot * sin[None, None]
            return jnp.concatenate([x_rot, x_pass], axis=-1)
        B, S, _ = hidden_states.shape
        G = H // KV
        qg = hidden_states @ Wq
        q, gate = (qg[..., :H * D], qg[..., H * D:])
        k = hidden_states @ Wk
        v = hidden_states @ Wv
        q = q.reshape(B, S, H, D).transpose(0, 2, 1, 3)
        k = k.reshape(B, S, KV, D).transpose(0, 2, 1, 3)
        v = v.reshape(B, S, KV, D).transpose(0, 2, 1, 3)
        cos, sin = _rope_cos_sin(S, q.dtype)
        q = _apply_partial_rope(q, cos, sin)
        k = _apply_partial_rope(k, cos, sin)
        qg4 = q.reshape(B, KV, G, S, D)
        scores = jnp.einsum('bkgsd,bktd->bkgst', qg4, k) / jnp.sqrt(jnp.asarray(D, q.dtype))
        attn = jax.nn.softmax(scores, axis=-1)
        out = jnp.einsum('bkgst,bktd->bkgsd', attn, v)
        out = out.reshape(B, H, S, D).transpose(0, 2, 1, 3).reshape(B, S, H * D)
        out = out * jax.nn.silu(gate)
        return out @ Wo

    def _L1_ffn_ref(x, gate_w, gate_b, w1, b1, w2, b2):
        import jax, jax.numpy as jnp
        import numpy as np
        B, S, D, H, O, E, K = (4, 256, 128, 256, 128, 8, 2)
        logits = jnp.einsum('bsd,ed->bse', x, gate_w) + gate_b
        probs = jax.nn.softmax(logits, axis=-1)
        topk_vals, topk_idx = jax.lax.top_k(probs, K)
        h = jax.nn.relu(jnp.einsum('bsd,edh->bseh', x, w1) + b1)
        expert_out = jnp.einsum('bseh,eho->bseo', h, w2) + b2
        sel = jnp.take_along_axis(expert_out, topk_idx[..., None], axis=2)
        return jnp.sum(sel * topk_vals[..., None], axis=2)
    x = L0_attn_x
    x = _layernorm(x + _L0_attn_ref(x, L0_attn_W0, L0_attn_b0, L0_attn_W1, L0_attn_b1), axis=-1)
    x = _layernorm(x + _L0_ffn_ref(x, L0_ffn_wg, L0_ffn_w1, L0_ffn_w3, L0_ffn_w2), axis=-1)
    x = _layernorm(x + _L1_attn_ref(x, L1_attn_Wq, L1_attn_Wk, L1_attn_Wv, L1_attn_Wo), axis=-1)
    x = _layernorm(x + _L1_ffn_ref(x, L1_ffn_gate_w, L1_ffn_gate_b, L1_ffn_w1, L1_ffn_b1, L1_ffn_w2, L1_ffn_b2), axis=-1)
    return x

_drawn_inputs = setup_inputs


def setup_inputs(seed=0):
    import zlib

    import numpy as np

    out = dict(_drawn_inputs(seed))
    spreads = {'L1_ffn_gate_b': (0.0, 0.1), 'L1_ffn_b1': (0.0, 0.1), 'L1_ffn_b2': (0.0, 0.1)}
    factors = {'L0_ffn_wg': 2.962,
     'L0_ffn_w1': 2.879,
     'L0_ffn_w3': 2.96,
     'L1_attn_Wq': 5.278,
     'L1_attn_Wk': 8.0,
     'L1_attn_Wv': 5.193,
     'L1_attn_Wo': 4.236}
    for name, (base, spread) in spreads.items():
        noise = np.random.default_rng([zlib.crc32(name.encode()), seed]).standard_normal(out[name].shape)
        drawn = base * np.exp(spread * noise) if base else spread * noise
        out[name] = jnp.asarray(drawn.astype(out[name].dtype))
    for name, factor in factors.items():
        out[name] = (out[name] * factor).astype(out[name].dtype)
    return out
```

```python
from contextlib import ExitStack

import numpy as np

import concourse.bass as bass
from concourse import mybir

F32 = mybir.dt.float32
F32R = mybir.dt.float32r
ALU = mybir.AluOpType
ACT = mybir.ActivationFunctionType
AX = mybir.AxisListType

P = 128
BATCH = 4
SEQ = 1024
CH = 512
NC = SEQ // CH
NT = SEQ // P
TPC = CH // P
E = 8
HALF = 2
UNITS = NC * E * HALF
HEADS, KV, HD = 8, 2, 32
G = HEADS // KV
ROT = HD // 4
RH = ROT // 2
NH = HEADS + KV
QKV = HEADS * HD + 2 * KV * HD
EPS = 1e-5
SCALE = float(HD) ** -0.5


def build_network(nc, d, out):
    ctx = ExitStack()
    with ctx:
        def sb(name, shape, dt=F32, scope=ctx):
            return scope.enter_context(nc.sbuf_tensor(name, shape, dt))

        def sem(name):
            return ctx.enter_context(nc.semaphore(name))

        ps = ctx.enter_context(nc.psum_tensor("ps", [P, 8, CH], F32))

        x_seq = sb("x_seq", [P, SEQ])
        gru_w = sb("gru_w", [P, 2, 2 * P])
        gru_b = sb("gru_b", [P, 2, 2])
        gru_nb = sb("gru_nb", [P, 2, 2])
        route_w = sb("route_w", [P, 2, E])
        route_b = sb("route_b", [P, E])
        up_w = [sb(f"up_w{i}", [P, 2, E * 2 * P], F32R) for i in range(2)]
        gate_up_w = sb("gate_up_w", [P, 2, E * 2 * P], F32R)
        down_w = [sb(f"down_w{i}", [P, 2, E * HALF * P], F32R) for i in range(2)]
        up_b = sb("up_b", [P, E * HALF])
        down_b = sb("down_b", [2 * E, P])
        qkv_w = sb("qkv_w", [P, QKV])
        ogate_w = sb("ogate_w", [P, HEADS * HD])
        out_w = sb("out_w", [P, KV, P])
        cos = sb("cos", [P, NT, RH])
        sin = sb("sin", [P, NT, RH])
        ident = sb("ident", [P, P])
        ones = sb("ones", [P, HD])
        rank = sb("rank", [P, E])
        pick = sb("pick", [2 * E, E, P], F32R)

        xT = sb("xT", [P, SEQ])
        resid = sb("resid", [P, SEQ])
        x_tok = sb("x_tok", [P, NT, P])
        stats = sb("stats", [P, NT, 6])
        mv = sb("mv", [P, NT, 2])
        var_eps = sb("var_eps", [P, NT])
        rstd = sb("rstd", [P, NT])
        minus_half = sb("minus_half", [P, TPC])
        r8 = [sb(f"r8_{i}", [P, NT, E]) for i in range(6)]
        r1 = [sb(f"r1_{i}", [P, NT]) for i in range(6)]
        wstack = sb("wstack", [P, NT, 2 * E], F32R)
        wT = sb("wT", [2 * E, SEQ], F32R)
        mpart = sb("mpart", [P, KV, G, NT, NC])
        mneg = sb("mneg", [P, KV, G * NT])
        mrow = sb("mrow", [G * NT, KV, P], F32R)
        with ExitStack() as scope:
            xh = sb("xh", [P, SEQ], F32R, scope)
            xl = sb("xl", [P, SEQ], F32R, scope)
        att = sb("att", [P, KV, SEQ])

        with ExitStack() as scope:
            kT = sb("kT", [3 * HD + 1, KV, SEQ], F32R, scope)
            qT = sb("qT", [3 * HD + 1, HEADS, SEQ], F32R, scope)
            gT = sb("gT", [P, KV, SEQ], F32, scope)
            qkv = sb("qkv", [P, NT, QKV], F32, scope)
            with ExitStack() as inner:
                stack = sb("stack", [P, TPC, NH, 3 * HD], F32R, inner)
                rope = [sb(f"rope{i}", [P, TPC, NH, RH], F32, inner) for i in range(4)]
            with ExitStack() as inner:
                NPB = 2
                prob = sb("prob", [P, NPB, G, CH], F32, inner)
                rden = sb("rden", [P, CH], F32, inner)
        with ExitStack() as scope:
            raw = sb("raw", [P, 2, E * 2 * P], F32, scope)
            pick_f = sb("pick_f", [2 * E, E, P], F32, scope)
        with ExitStack() as scope:
            g_a = sb("g_a", [P, 2, CH], F32, scope)
            g_z = sb("g_z", [P, 2, CH], F32, scope)
            g_s = sb("g_s", [P, 2, CH], F32, scope)
            g_r = sb("g_r", [P, CH], F32, scope)
            g_g = sb("g_g", [P, CH], F32, scope)
            g_v = sb("g_v", [P, CH], F32, scope)
            hid = sb("hid", [P, 2, SEQ], F32, scope)
        with ExitStack() as scope:
            NB = 4
            e_u = sb("e_u", [P, NB, CH], F32, scope)
            e_t = sb("e_t", [P, CH], F32, scope)
            e_h = sb("e_h", [P, NB, CH], F32, scope)
            e_hh = sb("e_hh", [P, NB, CH], F32R, scope)
            e_hl = sb("e_hl", [P, NB, CH], F32R, scope)

        x_in, small_in = sem("x_in"), sem("small_in")
        raw_in = [sem("raw_in0"), sem("raw_in1")]
        hi_made, lo_made = sem("hi_made"), sem("lo_made")
        const_made, vec_const = sem("const_made"), sem("vec_const")
        names = """gru_mm gru_gates gru_state vec_step norm_in norm_turned norm_var norm_rstd norm_done norm_back
            xT_made xh_made xl_made
            route_mm route_logit route_exp route_weight route_turned route_wT
            mix0_mm mix0_act mix0_h mix0_hi mix0_lo mix0_down
            mix1_mm mix1_act mix1_h mix1_hi mix1_lo mix1_down
            qkv_mm qkv_read rope_done stack_act stack_vec head_turned headT_act headT_vec
            ogate_mm ogate_done max_mm max_red max_neg mrow_turned mrow_made mrow_placed
            score_mm prob_made pv_mm pv_read att_made wo_mm out_stored next_in ones_row""".split()
        s = {n: sem(n) for n in names}

        raws = [("up0", up_w[0]), ("gate_up", gate_up_w), ("down0", down_w[0]),
                ("up1", up_w[1]), ("down1", down_w[1])]
        with nc.Block() as block:
            @block.sync
            def _(sp):
                sp.dma_start(x_seq[:], d["xT"][0]).then_inc(x_in, 16)
                small = [(gru_w[:], d["gru_w"]), (gru_b[:], d["gru_b"]), (route_w[:], d["route_w"]),
                         (route_b[:], d["route_b"]), (up_b[:], d["up_b"]), (down_b[:], d["down_b"]),
                         (qkv_w[:], d["qkv_w"]), (ogate_w[:], d["ogate_w"]), (out_w[:], d["out_w"]),
                         (cos[:], d["cos"]), (sin[:], d["sin"])]
                for to, of in small:
                    sp.dma_start(to, of).then_inc(small_in, 16)
                for n, (name, _) in enumerate(raws):
                    if n >= 2:
                        sp.wait_ge(hi_made, n - 1)
                        sp.wait_ge(lo_made, n - 1)
                    sp.dma_start(raw[:, n % 2], d[name]).then_inc(raw_in[n % 2], 16)
                sp.wait_ge(x_in, 16)
                sp.wait_ge(small_in, 16 * len(small))

            @block.scalar
            def _(act):
                for n, (_, w) in enumerate(raws):
                    act.wait_ge(raw_in[n % 2], 16 * (n // 2 + 1))
                    act.activation(w[:, 0], raw[:, n % 2], ACT.Copy).then_inc(hi_made, 1)

            @block.vector
            def _(vec):
                vec.memset(ones[:], 1.0)
                vec.memset(minus_half[:], -0.5)
                for e in range(E):
                    vec.memset(rank[:, e:e + 1], float(E - e))
                vec.wait_ge(const_made, 3)
                vec.tensor_copy(pick[:], pick_f[:]).then_inc(vec_const, 1)
                vec.wait_ge(small_in, 16 * 11)
                vec.tensor_scalar(gru_nb[:], gru_b[:], -1.0, None, ALU.mult).then_inc(vec_const, 1)
                for n, (_, w) in enumerate(raws):
                    vec.wait_ge(hi_made, n + 1)
                    vec.tensor_tensor(w[:, 1], raw[:, n % 2], w[:, 0].bitcast(F32), ALU.subtract)\
                       .then_inc(lo_made, 1)
                vec.wait_ge(vec_const, 2)

            @block.gpsimd
            def _(pool):
                pool.memset(ident[:], 0.0).then_inc(const_made, 1)
                pool.wait_ge(const_made, 1)
                pool.affine_select(out=ident[:], in_=ident[:], compare_op=ALU.not_equal, fill=1.0,
                                   base=0, pattern=[[-1, P]], channel_multiplier=1)
                pool.memset(pick_f[:], 0.0).then_inc(const_made, 1)
                pool.wait_ge(const_made, 2)
                step = sem("pick_step")
                pool.affine_select(out=pick_f[:], in_=pick_f[:], compare_op=ALU.not_equal, fill=1.0,
                                   base=0, pattern=[[-1, E], [0, P]], channel_multiplier=1).then_inc(step, 1)
                pool.wait_ge(step, 1)
                pool.affine_select(out=pick_f[:], in_=pick_f[:], compare_op=ALU.not_equal, fill=1.0,
                                   base=-E, pattern=[[-1, E], [0, P]], channel_multiplier=1)\
                    .then_inc(const_made, 1)

        with nc.Fori(0, BATCH) as b:
            with nc.Block() as block:
                @block.tensor
                def _(pe):
                    def mm3(to, w, wslice, xhi, xlo, start=True, stop=True):
                        pe.matmul(to, w[:, 0, wslice], xhi, start=start, stop=False)
                        pe.matmul(to, w[:, 1, wslice], xhi, start=False, stop=False)
                        return pe.matmul(to, w[:, 0, wslice], xlo, start=False, stop=stop)

                    def gru():
                        for k in range(2 * NC):
                            layer, c = divmod(k, NC)
                            if k >= 2:
                                pe.wait_ge(s["gru_state"], k - 1)
                            rhs = x_seq[:, c * CH:(c + 1) * CH] if layer == 0 else hid[:, 0, c * CH:(c + 1) * CH]
                            for j in range(2):
                                mm = pe.matmul(ps[:, 2 * (k % 2) + j], gru_w[:, layer, j * P:(j + 1) * P],
                                               rhs, start=True, stop=True)
                            mm.then_inc(s["gru_mm"], 1)

                    def norm(i):
                        for c in range(NC):
                            pe.wait_ge(s["norm_in"], NC * i + c + 1)
                            for t in range(TPC * c, TPC * (c + 1)):
                                mm = pe.transpose(ps[:, 4 + c, (t % TPC) * P:(t % TPC + 1) * P],
                                                  resid[:, t * P:(t + 1) * P], ident[:])
                            mm.then_inc(s["norm_turned"], 1)
                        if i == 3:
                            return
                        for c in range(NC):
                            pe.wait_ge(s["norm_done"], NC * i + c + 1)
                            for t in range(TPC * c, TPC * (c + 1)):
                                mm = pe.transpose(ps[:, 6 + c, (t % TPC) * P:(t % TPC + 1) * P],
                                                  x_tok[:, t], ident[:])
                            mm.then_inc(s["norm_back"], 1)

                    def route(i, n):
                        pe.wait_ge(s["xT_made"], NC * (n + 1))
                        for t in range(NT):
                            mm = pe.matmul(ps[:, 0, t * E:(t + 1) * E], xT[:, t * P:(t + 1) * P],
                                           route_w[:, i], start=True, stop=True)
                        mm.then_inc(s["route_mm"], 1)
                        pe.wait_ge(s["route_weight"], i + 1)
                        for t in range(NT):
                            mm = pe.transpose(ps[0:2 * E, 1 + t // TPC, (t % TPC) * P:(t % TPC + 1) * P],
                                              wstack[:, t].bitcast(F32), ident[:])
                        mm.then_inc(s["route_turned"], 1)
                        pe.wait_ge(s["route_wT"], i + 1)
                        pe.wait_ge(s["xh_made"], NC * (n + 1 - i))
                        pe.wait_ge(s["xl_made"], NC * (n + 1 - i))

                    def spread(i, c, e):
                        m = c * E + e
                        if m >= 2:
                            pe.wait_ge(s[f"mix{i}_h"], 2 * (m - 1))
                        pe.matmul(ps[:, 4 + m % 2], pick[:, e], wT[:, c * CH:(c + 1) * CH],
                                  start=True, stop=True)

                    def down(i, n):
                        c, e, h = n // (E * HALF), n // HALF % E, n % HALF
                        pe.wait_ge(s[f"mix{i}_hi"], n + 1)
                        pe.wait_ge(s[f"mix{i}_lo"], n + 1)
                        first = i == 0 and n % (E * HALF) == 0
                        k = (e * HALF + h) * P
                        mm3(ps[:, 6 + c], down_w[i], slice(k, k + P), e_hh[:, n % NB], e_hl[:, n % NB],
                            start=first, stop=n % (E * HALF) == E * HALF - 1)\
                            .then_inc(s[f"mix{i}_down"], 1)

                    LAG = 2

                    def mix0():
                        for n in range(UNITS + LAG):
                            if n < UNITS:
                                c, e, h = n // (E * HALF), n // HALF % E, n % HALF
                                if h == 0:
                                    spread(0, c, e)
                                if n >= 2:
                                    pe.wait_ge(s["mix0_h"], n - 1)
                                k = (e * HALF + h) * P
                                tok = slice(c * CH, (c + 1) * CH)
                                mm3(ps[:, 2 * (n % 2)], up_w[0], slice(k, k + P), xh[:, tok], xl[:, tok])
                                mm3(ps[:, 2 * (n % 2) + 1], gate_up_w, slice(k, k + P), xh[:, tok], xl[:, tok])\
                                    .then_inc(s["mix0_mm"], 1)
                            if n >= LAG:
                                down(0, n - LAG)

                    def mix1():
                        for n in range(UNITS + LAG):
                            if n < UNITS:
                                c, e, h = n // (E * HALF), n // HALF % E, n % HALF
                                tok = slice(c * CH, (c + 1) * CH)
                                if h == 0:
                                    spread(1, c, e)
                                if n % (E * HALF) == 0:
                                    pe.matmul(ps[:, 6 + c], down_b[:], wT[:, tok].bitcast(F32),
                                              start=True, stop=False)
                                if n >= 4:
                                    pe.wait_ge(s["mix1_act"], n - 3)
                                k = (e * HALF + h) * P
                                mm3(ps[:, n % 4], up_w[1], slice(k, k + P), xh[:, tok], xl[:, tok])\
                                    .then_inc(s["mix1_mm"], 1)
                            if n >= LAG:
                                down(1, n - LAG)

                    def project():
                        for t in range(NT):
                            if t >= 2:
                                pe.wait_ge(s["qkv_read"], t - 1)
                            pe.matmul(ps[:, t % 2, 0:QKV], xT[:, t * P:(t + 1) * P], qkv_w[:],
                                      start=True, stop=True).then_inc(s["qkv_mm"], 1)
                        for k in range(KV * NC):
                            g, c = divmod(k, NC)
                            if k >= 2:
                                pe.wait_ge(s["ogate_done"], k - 1)
                            pe.matmul(ps[:, 2 + k % 2], ogate_w[:, g * P:(g + 1) * P],
                                      xT[:, c * CH:(c + 1) * CH], start=True, stop=True)\
                              .then_inc(s["ogate_mm"], 1)

                    def turn_heads():
                        for c in range(NC):
                            pe.wait_ge(s["stack_act"], c + 1)
                            pe.wait_ge(s["stack_vec"], c + 1)
                            for h in range(NH):
                                n = c * NH + h
                                if n >= 4:
                                    pe.wait_ge(s["headT_vec" if n % 2 else "headT_act"], (n - 4) // 2 + 1)
                                for t in range(TPC):
                                    mm = pe.transpose(ps[0:3 * HD, 4 + n % 4, t * P:(t + 1) * P],
                                                      stack[:, t, h].bitcast(F32), ident[:])
                                mm.then_inc(s["head_turned"], 1)

                    def max_scores(g, u):
                        j, t, c = u // (NT * NC), u // NC % NT, u % NC
                        m = g * G * NT * NC + u
                        if m >= 2:
                            pe.wait_ge(s["max_red"], m - 1)
                        pe.matmul(ps[:, m % 2], qT[0:3 * HD, g * G + j, t * P:(t + 1) * P],
                                  kT[0:3 * HD, g, c * CH:(c + 1) * CH], start=True, stop=True)\
                          .then_inc(s["max_mm"], 1)

                    def turn_max(g):
                        pe.wait_ge(s["max_neg"], g + 1)
                        pe.transpose(ps[0:G * NT, 0, 0:P], mneg[:, g], ident[:]).then_inc(s["mrow_turned"], 1)

                    def scores(k):
                        g, c, t = k // (NC * NT), k // NT % NC, k % NT
                        for p in range(G // 2):
                            n = k * (G // 2) + p
                            if n >= 2:
                                pe.wait_ge(s["prob_made"], n - 1)
                            for j in range(2):
                                mm = pe.matmul(ps[:, 4 + 2 * (n % 2) + j], kT[:, g, t * P:(t + 1) * P],
                                               qT[:, g * G + 2 * p + j, c * CH:(c + 1) * CH],
                                               start=True, stop=True)
                            mm.then_inc(s["score_mm"], 1)

                    def values(k):
                        g, gc, t = k // (NC * NT), k // NT, k % NT
                        pe.wait_ge(s["prob_made"], (G // 2) * (k + 1))
                        if t == 0 and gc >= 1:
                            pe.wait_ge(s["pv_read"], gc)
                        v0 = (HEADS + KV) * HD + g * HD
                        for bank, w in ((2, qkv[:, t, v0:v0 + HD]), (3, ones[:])):
                            for j in range(G):
                                mm = pe.matmul(ps[j * HD:(j + 1) * HD, bank], w, prob[:, k % NPB, j],
                                               start=t == 0, stop=t == NT - 1)
                        mm.then_inc(s["pv_mm"], 1)

                    def attend():
                        units = G * NT * NC
                        pe.wait_ge(s["headT_act"], NC * NH // 2)
                        pe.wait_ge(s["headT_vec"], NC * NH // 2)
                        for u in range(units):
                            max_scores(0, u)
                        turn_max(0)
                        pe.wait_ge(s["ones_row"], 1)
                        per = units // (NC * NT)
                        for k in range(KV * NC * NT):
                            if k % (NC * NT) == 0:
                                pe.wait_ge(s["mrow_placed"], 16 * (k // (NC * NT) + 1))
                            scores(k)
                            if k < NC * NT:
                                if k == 0:
                                    pe.wait_ge(s["mrow_made"], 1)
                                for u in range(per * k, per * (k + 1)):
                                    max_scores(1, u)
                            if k == NC * NT - 1:
                                turn_max(1)
                            if k >= 1:
                                values(k - 1)
                        values(KV * NC * NT - 1)
                        pe.wait_ge(s["att_made"], KV * NC)
                        for c in range(NC):
                            for g in range(KV):
                                mm = pe.matmul(ps[:, c], out_w[:, g], att[:, g, c * CH:(c + 1) * CH],
                                               start=g == 0, stop=g == KV - 1)
                            mm.then_inc(s["wo_mm"], 1)

                    gru()
                    norm(0)
                    route(0, 0)
                    mix0()
                    norm(1)
                    pe.wait_ge(s["xT_made"], 2 * NC)
                    project()
                    turn_heads()
                    attend()
                    norm(2)
                    route(1, 2)
                    mix1()
                    norm(3)

                @block.scalar
                def _(act):
                    def gru():
                        for k in range(2 * NC):
                            layer, i = k // NC, k % 2
                            act.wait_ge(s["gru_mm"], k + 1)
                            if k >= 2:
                                act.wait_ge(s["gru_state"], k - 1)
                            act.activation(g_s[:, i], ps[:, 2 * i + 1], ACT.Sigmoid,
                                           bias=gru_b[:, layer, 1:2]).then_inc(s["gru_gates"], 1)
                            act.activation(g_z[:, i], ps[:, 2 * i], ACT.Sigmoid,
                                           bias=gru_b[:, layer, 0:1]).then_inc(s["gru_gates"], 1)
                            act.activation(g_a[:, i], ps[:, 2 * i], ACT.Sigmoid, scale=-1.0,
                                           bias=gru_nb[:, layer, 0:1]).then_inc(s["gru_gates"], 1)

                    def norm(i):
                        for c in range(NC):
                            tok = slice(c * CH, (c + 1) * CH)
                            act.wait_ge(s["norm_back"], NC * i + c + 1)
                            if i != 1:
                                act.activation(xh[:, tok], ps[:, 6 + c], ACT.Copy).then_inc(s["xh_made"], 1)
                            act.activation(xT[:, tok], ps[:, 6 + c], ACT.Copy).then_inc(s["xT_made"], 1)

                    def route(i):
                        act.wait_ge(s["route_logit"], i + 1)
                        act.activation(r8[1][:], r8[0][:], ACT.Exp).then_inc(s["route_exp"], 1)
                        act.wait_ge(s["route_turned"], i + 1)
                        act.activation(wT[:].rearrange("p (a b) -> p a b", a=NC), ps[0:2 * E, 1:1 + NC], ACT.Copy)\
                           .then_inc(s["route_wT"], 1)

                    def hi(i, n):
                        act.wait_ge(s[f"mix{i}_h"], n + 1)
                        if n >= NB:
                            act.wait_ge(s[f"mix{i}_down"], n - NB + 1)
                        act.activation(e_hh[:, n % NB], e_h[:, n % NB], ACT.Copy).then_inc(s[f"mix{i}_hi"], 1)

                    def mix0():
                        for n in range(UNITS + 1):
                            if n < UNITS:
                                act.wait_ge(s["mix0_mm"], n + 1)
                                if n >= NB:
                                    act.wait_ge(s["mix0_h"], n - NB + 1)
                                act.activation(e_u[:, n % NB], ps[:, 2 * (n % 2)], ACT.Silu)\
                                   .then_inc(s["mix0_act"], 1)
                            if n >= 1:
                                hi(0, n - 1)

                    def mix1():
                        for n in range(UNITS + 1):
                            if n < UNITS:
                                eh = n % (E * HALF)
                                act.wait_ge(s["mix1_mm"], n + 1)
                                if n >= NB:
                                    act.wait_ge(s["mix1_h"], n - NB + 1)
                                act.activation(e_u[:, n % NB], ps[:, n % 4], ACT.Relu, bias=up_b[:, eh:eh + 1])\
                                   .then_inc(s["mix1_act"], 1)
                            if n >= 1:
                                hi(1, n - 1)

                    def project():
                        for t in range(NT):
                            act.wait_ge(s["qkv_mm"], t + 1)
                            act.activation(qkv[:, t], ps[:, t % 2, 0:QKV], ACT.Copy).then_inc(s["qkv_read"], 1)
                        for k in range(KV * NC):
                            g, c = divmod(k, NC)
                            act.wait_ge(s["ogate_mm"], k + 1)
                            act.activation(gT[:, g, c * CH:(c + 1) * CH], ps[:, 2 + k % 2], ACT.Silu)\
                               .then_inc(s["ogate_done"], 1)

                    def heads():
                        for c in range(NC):
                            act.wait_ge(s["rope_done"], c + 1)
                            if c >= 1:
                                act.wait_ge(s["head_turned"], c * NH)
                            src = qkv[:, c * TPC:(c + 1) * TPC, 0:NH * HD].rearrange("p t (h f) -> p t h f", f=HD)
                            act.activation(stack[:, :, :, 0:HD], src, ACT.Copy).then_inc(s["stack_act"], 1)
                            for h in range(0, NH, 2):
                                n = c * NH + h
                                act.wait_ge(s["head_turned"], n + 1)
                                to = qT[0:3 * HD, h] if h < HEADS else kT[0:3 * HD, h - HEADS]
                                act.activation(to[:, c * CH:(c + 1) * CH], ps[0:3 * HD, 4 + n % 4], ACT.Copy)\
                                   .then_inc(s["headT_act"], 1)

                    def attend():
                        for n in range(KV * NC * NT * (G // 2)):
                            k, p = divmod(n, G // 2)
                            act.wait_ge(s["score_mm"], n + 1)
                            if k >= NPB:
                                act.wait_ge(s["pv_mm"], k - NPB + 1)
                            act.activation(prob[:, k % NPB, 2 * p:2 * p + 2],
                                           ps[:, 4 + 2 * (n % 2):6 + 2 * (n % 2)], ACT.Exp, scale=SCALE)\
                               .then_inc(s["prob_made"], 1)

                    gru()
                    norm(0)
                    route(0)
                    mix0()
                    norm(1)
                    project()
                    heads()
                    attend()
                    norm(2)
                    route(1)
                    mix1()

                @block.vector
                def _(vec):
                    steps = [0]

                    def then(ins):
                        steps[0] += 1
                        ins.then_inc(s["vec_step"], 1)
                        vec.wait_ge(s["vec_step"], steps[0])

                    def gru():
                        for k in range(2 * NC):
                            layer, c = divmod(k, NC)
                            i = k % 2
                            vec.wait_ge(s["gru_gates"], 3 * k + 1)
                            then(vec.tensor_scalar(g_r[:], ps[:, 2 * i + 1], gru_b[:, layer, 1:2], 0.0,
                                                   ALU.add, ALU.max))
                            vec.wait_ge(s["gru_gates"], 3 * k + 3)
                            then(vec.scalar_tensor_tensor(g_g[:], g_s[:, i], 0.5, g_r[:], ALU.min, ALU.add))
                            then(vec.tensor_tensor(g_v[:], g_z[:, i], g_g[:], ALU.mult))
                            h = hid[:, layer]
                            first = 0.5 if c == 0 else h[:, c * CH - 1:c * CH]
                            vec.tensor_tensor_scan(h[:, c * CH:(c + 1) * CH], g_a[:, i], g_v[:], first,
                                                   ALU.mult, ALU.add).then_inc(s["gru_state"], 1)
                            vec.wait_ge(s["gru_state"], k + 1)
                            if layer == 1:
                                vec.tensor_tensor(resid[:, c * CH:(c + 1) * CH], x_seq[:, c * CH:(c + 1) * CH],
                                                  h[:, c * CH:(c + 1) * CH], ALU.add).then_inc(s["norm_in"], 1)

                    def norm(i):
                        for c in range(NC):
                            vec.wait_ge(s["norm_turned"], NC * i + c + 1)
                            ts = range(TPC * c, TPC * (c + 1))
                            tile = lambda t: ps[:, 4 + c, (t % TPC) * P:(t % TPC + 1) * P]
                            for t in ts:
                                last = vec.bn_stats(stats[:, t], tile(t))
                            then(last)
                            for t in ts:
                                last = vec.bn_aggr(mv[:, t], stats[:, t])
                            then(last)
                            cs = slice(TPC * c, TPC * (c + 1))
                            vec.tensor_scalar(var_eps[:, cs], mv[:, cs, 1], EPS, None, ALU.add)\
                               .then_inc(s["norm_var"], 1)
                            vec.wait_ge(s["norm_rstd"], NC * i + c + 1)
                            for t in ts:
                                last = vec.tensor_scalar(x_tok[:, t], tile(t), mv[:, t, 0:1], rstd[:, t:t + 1],
                                                         ALU.subtract, ALU.mult)
                            last.then_inc(s["norm_done"], 1)
                        if i == 3:
                            return
                        if i != 1:
                            for c in range(NC):
                                tok = slice(c * CH, (c + 1) * CH)
                                vec.wait_ge(s["xT_made"], NC * i + c + 1)
                                vec.tensor_tensor(xl[:, tok], xT[:, tok], xh[:, tok].bitcast(F32),
                                                  ALU.subtract).then_inc(s["xl_made"], 1)

                    def over(x):
                        return x.rearrange("p (t e) -> p t e", e=1).broadcast_to([P, NT, E])

                    def route(i):
                        lg, ex, pr, eq, oh1, oh2 = (r[:] for r in r8)
                        mx, sm, m1, v, m2, tmp = (r[:] for r in r1)
                        vec.wait_ge(s["route_mm"], i + 1)
                        got = ps[:, 0, 0:NT * E].rearrange("p (t e) -> p t e", e=E)
                        if i == 0:
                            then(vec.tensor_copy(pr, got))
                        else:
                            bias = route_b[:].rearrange("p (t e) -> p t e", t=1).broadcast_to([P, NT, E])
                            then(vec.tensor_tensor(pr, got, bias, ALU.add))
                        then(vec.tensor_reduce(mx, pr, AX.X, ALU.max))
                        vec.tensor_tensor(lg, pr, over(mx), ALU.subtract).then_inc(s["route_logit"], 1)
                        vec.wait_ge(s["route_exp"], i + 1)
                        then(vec.tensor_reduce(sm, ex, AX.X, ALU.add))
                        then(vec.reciprocal(tmp, sm))
                        then(vec.tensor_tensor(pr, ex, over(tmp), ALU.mult))
                        ranks = rank[:].rearrange("p (t e) -> p t e", t=1).broadcast_to([P, NT, E])

                        def first_of(x, m, oh):
                            then(vec.tensor_reduce(m, x, AX.X, ALU.max))
                            then(vec.tensor_tensor(eq, x, over(m), ALU.is_equal))
                            then(vec.tensor_tensor(eq, eq, ranks, ALU.mult))
                            then(vec.tensor_reduce(v, eq, AX.X, ALU.max))
                            then(vec.tensor_tensor(oh, eq, over(v), ALU.is_equal))

                        first_of(pr, m1, oh1)
                        then(vec.scalar_tensor_tensor(ex, oh1, -2.0, pr, ALU.mult, ALU.add))
                        first_of(ex, m2, oh2)
                        then(vec.tensor_tensor(oh1, oh1, oh2, ALU.add))
                        then(vec.tensor_tensor(pr, pr, oh1, ALU.mult))
                        if i == 0:
                            then(vec.tensor_tensor(sm, m1, m2, ALU.add))
                            then(vec.reciprocal(tmp, sm))
                            then(vec.tensor_tensor(pr, pr, over(tmp), ALU.mult))
                        then(vec.tensor_copy(wstack[:, :, 0:E], pr))
                        vec.tensor_tensor(wstack[:, :, E:2 * E], pr, wstack[:, :, 0:E].bitcast(F32),
                                          ALU.subtract).then_inc(s["route_weight"], 1)

                    def mix0():
                        for n in range(UNITS):
                            c, m = n // (E * HALF), n // HALF
                            vec.wait_ge(s["mix0_act"], n + 1)
                            then(vec.tensor_tensor(e_t[:], e_u[:, n % NB], ps[:, 4 + m % 2], ALU.mult))
                            if n >= NB:
                                vec.wait_ge(s["mix0_lo"], n - NB + 1)
                            vec.tensor_tensor(e_h[:, n % NB], e_t[:], ps[:, 2 * (n % 2) + 1], ALU.mult)\
                               .then_inc(s["mix0_h"], 1)
                            vec.wait_ge(s["mix0_h"], n + 1)
                            add_down(0, n)

                    def mix1():
                        for n in range(UNITS):
                            m = n // HALF
                            vec.wait_ge(s["mix1_act"], n + 1)
                            if n >= NB:
                                vec.wait_ge(s["mix1_lo"], n - NB + 1)
                            vec.tensor_tensor(e_h[:, n % NB], e_u[:, n % NB], ps[:, 4 + m % 2], ALU.mult)\
                               .then_inc(s["mix1_h"], 1)
                            add_down(1, n)

                    def add_down(i, n):
                        for c in range(NC):
                            if n == min(E * HALF * (c + 1) + 3, UNITS - 1):
                                tok = slice(c * CH, (c + 1) * CH)
                                vec.wait_ge(s[f"mix{i}_down"], E * HALF * (c + 1))
                                vec.tensor_tensor(resid[:, tok], xT[:, tok], ps[:, 6 + c], ALU.add)\
                                   .then_inc(s["norm_in"], 1)

                    def heads():
                        for c in range(NC):
                            cs = slice(c * TPC, (c + 1) * TPC)
                            vec.wait_ge(s["qkv_read"], TPC * (c + 1))
                            x = qkv[:, cs, 0:NH * HD].rearrange("p t (h f) -> p t h f", f=HD)
                            x1, x2 = x[:, :, :, 0:RH], x[:, :, :, RH:ROT]
                            co, si = (w[:, cs].rearrange("p t (h f) -> p t h f", h=1)
                                      .broadcast_to([P, TPC, NH, RH]) for w in (cos, sin))
                            a, b_, c_, d_ = (r[:] for r in rope)
                            vec.tensor_tensor(a, x1, co, ALU.mult)
                            vec.tensor_tensor(b_, x2, si, ALU.mult)
                            vec.tensor_tensor(c_, x2, co, ALU.mult)
                            then(vec.tensor_tensor(d_, x1, si, ALU.mult))
                            vec.tensor_tensor(x1, a, b_, ALU.subtract)
                            vec.tensor_tensor(x2, c_, d_, ALU.add).then_inc(s["rope_done"], 1)
                            vec.wait_ge(s["rope_done"], c + 1)
                            vec.wait_ge(s["stack_act"], c + 1)
                            q, k = slice(0, HEADS), slice(HEADS, NH)
                            hi = stack[:, :, :, 0:HD].bitcast(F32)
                            vec.tensor_tensor(stack[:, :, q, HD:2 * HD], x[:, :, q], hi[:, :, q], ALU.subtract)
                            vec.tensor_tensor(stack[:, :, k, 2 * HD:3 * HD], x[:, :, k], hi[:, :, k], ALU.subtract)
                            vec.tensor_copy(stack[:, :, q, 2 * HD:3 * HD], hi[:, :, q])
                            vec.tensor_copy(stack[:, :, k, HD:2 * HD], hi[:, :, k]).then_inc(s["stack_vec"], 1)
                            for h in range(1, NH, 2):
                                n = c * NH + h
                                vec.wait_ge(s["head_turned"], n + 1)
                                to = qT[0:3 * HD, h] if h < HEADS else kT[0:3 * HD, h - HEADS]
                                vec.tensor_copy(to[:, c * CH:(c + 1) * CH], ps[0:3 * HD, 4 + n % 4])\
                                   .then_inc(s["headT_vec"], 1)

                    def maxima(g, u):
                        j, t, c = u // (NT * NC), u // NC % NT, u % NC
                        m = g * G * NT * NC + u
                        vec.wait_ge(s["max_mm"], m + 1)
                        vec.tensor_reduce(mpart[:, g, j, t, c:c + 1], ps[:, m % 2], AX.X, ALU.max)\
                           .then_inc(s["max_red"], 1)

                    def negate(g):
                        vec.wait_ge(s["max_red"], (g + 1) * G * NT * NC)
                        vec.tensor_reduce(mneg[:, g], mpart[:, g].rearrange("p j t c -> p (j t) c"),
                                          AX.X, ALU.max, negate=True).then_inc(s["max_neg"], 1)
                        vec.wait_ge(s["mrow_turned"], g + 1)
                        vec.tensor_copy(mrow[:, g], ps[0:G * NT, 0, 0:P]).then_inc(s["mrow_made"], 1)

                    def gated(gc):
                        g, c = divmod(gc, NC)
                        to = att[:, g, c * CH:(c + 1) * CH]
                        vec.wait_ge(s["pv_mm"], NT * (gc + 1))
                        then(vec.reciprocal(rden[:], ps[:, 3]))
                        vec.tensor_tensor(to, ps[:, 2], rden[:], ALU.mult).then_inc(s["pv_read"], 1)
                        vec.wait_ge(s["pv_read"], gc + 1)
                        vec.tensor_tensor(to, to, gT[:, g, c * CH:(c + 1) * CH], ALU.mult)\
                           .then_inc(s["att_made"], 1)

                    def attend():
                        units = G * NT * NC
                        for u in range(units):
                            maxima(0, u)
                        negate(0)
                        for u in range(units):
                            maxima(1, u)
                            if u == G * (NT + 1) - 1:
                                gated(0)
                        negate(1)
                        for gc in range(1, KV * NC):
                            gated(gc)
                        for c in range(NC):
                            tok = slice(c * CH, (c + 1) * CH)
                            vec.wait_ge(s["wo_mm"], c + 1)
                            vec.tensor_tensor(resid[:, tok], xT[:, tok], ps[:, c], ALU.add)\
                               .then_inc(s["norm_in"], 1)

                    gru()
                    norm(0)
                    route(0)
                    mix0()
                    norm(1)
                    heads()
                    attend()
                    norm(2)
                    route(1)
                    mix1()
                    norm(3)

                @block.gpsimd
                def _(pool):
                    def norm(i):
                        for c in range(NC):
                            cs = slice(TPC * c, TPC * (c + 1))
                            pool.wait_ge(s["norm_var"], NC * i + c + 1)
                            pool.tensor_tensor(rstd[:, cs], var_eps[:, cs], minus_half[:], ALU.pow)\
                                .then_inc(s["norm_rstd"], 1)

                    for i in range(2):
                        norm(2 * i)
                        for n in range(UNITS):
                            pool.wait_ge(s[f"mix{i}_hi"], n + 1)
                            if n >= NB:
                                pool.wait_ge(s[f"mix{i}_down"], n - NB + 1)
                            pool.tensor_tensor(e_hl[:, n % NB], e_h[:, n % NB], e_hh[:, n % NB].bitcast(F32),
                                               ALU.subtract).then_inc(s[f"mix{i}_lo"], 1)
                        if i == 0:
                            pool.wait_ge(s["norm_in"], 2 * NC)
                            pool.memset(kT[3 * HD:3 * HD + 1].bitcast(F32), 1.0).then_inc(s["ones_row"], 1)
                            pool.wait_ge(s["ones_row"], 1)
                        norm(2 * i + 1)

                @block.sync
                def _(sp):
                    sp.wait_ge(s["norm_in"], NC)
                    sp.dma_start(x_seq[:], d["xT"][(b + 1) % BATCH]).then_inc(s["next_in"], 16)
                    for g in range(KV):
                        sp.wait_ge(s["mrow_made"], g + 1)
                        sp.dma_start(qT[3 * HD:3 * HD + 1, g * G:(g + 1) * G, :].bitcast(F32), mrow[:, g].bitcast(F32))\
                          .then_inc(s["mrow_placed"], 16)
                    for c in range(NC):
                        sp.wait_ge(s["norm_done"], 3 * NC + c + 1)
                        sp.dma_start(out[b, c], x_tok[:, c * TPC:(c + 1) * TPC]).then_inc(s["out_stored"], 16)
                    sp.wait_ge(s["out_stored"], 16 * NC)
                    sp.wait_ge(s["next_in"], 16)

            with nc.Block() as block:
                @block.sync
                def _(sp):
                    for n in names:
                        sp.sem_clear(s[n])


def rotary_table():
    inv = (1.0 / np.float32(10000.0) ** (np.arange(0, ROT, 2, dtype=np.float32) / np.float32(ROT)))
    freqs = np.arange(SEQ, dtype=np.float32)[:, None] * inv.astype(np.float32)[None, :]
    split = lambda a: np.ascontiguousarray(a.astype(np.float32).reshape(NT, P, RH).transpose(1, 0, 2))
    return split(np.cos(freqs)), split(np.sin(freqs))


def lay_out(a):
    t = np.ascontiguousarray
    cos, sin = rotary_table()
    by_partition = lambda w: t(w.reshape(-1, HALF, P, P).transpose(2, 0, 1, 3).reshape(P, -1))
    wq, wk, wv = a["L1_attn_Wq"], a["L1_attn_Wk"], a["L1_attn_Wv"]
    return {
        "xT": t(a["L0_attn_x"].transpose(0, 2, 1)),
        "gru_w": t(np.stack([a["L0_attn_W0"].T, a["L0_attn_W1"].T], 1)),
        "gru_b": t(np.stack([a["L0_attn_b0"].reshape(2, P).T, a["L0_attn_b1"].reshape(2, P).T], 1)),
        "route_w": t(np.stack([a["L0_ffn_wg"].T, a["L1_ffn_gate_w"].T], 1)),
        "route_b": t(np.repeat(a["L1_ffn_gate_b"][None], P, 0)),
        "up0": t(a["L0_ffn_w1"].transpose(2, 0, 1).reshape(P, -1)),
        "gate_up": t(a["L0_ffn_w3"].transpose(2, 0, 1).reshape(P, -1)),
        "down0": by_partition(a["L0_ffn_w2"].transpose(0, 2, 1)),
        "up1": t(a["L1_ffn_w1"].transpose(1, 0, 2).reshape(P, -1)),
        "down1": by_partition(a["L1_ffn_w2"]),
        "up_b": t(a["L1_ffn_b1"].reshape(E * HALF, P).T),
        "down_b": t(np.concatenate([a["L1_ffn_b2"]] * 2, 0)),
        "qkv_w": t(np.concatenate([wq[:, :HEADS * HD], wk, wv], 1)),
        "ogate_w": t(wq[:, HEADS * HD:]),
        "out_w": t(a["L1_attn_Wo"].reshape(KV, P, P).transpose(1, 0, 2)),
        "cos": cos,
        "sin": sin,
    }


def kernel(**inputs):
    import concourse.bacc as _bacc
    from concourse.bass_utils import run_bass_kernel_spmd as _run

    arrays = lay_out({k: np.asarray(v) for k, v in inputs.items()})
    nc = _bacc.Bacc("TRN2", target_bir_lowering=False, num_devices=1)
    ins = {k: nc.dram_tensor(f"in_{k}", v.shape, mybir.dt.from_np(v.dtype), kind="ExternalInput").ap()
           for k, v in arrays.items()}
    out = nc.dram_tensor("out", (BATCH, SEQ, P), F32, kind="ExternalOutput").ap()
    build_network(nc, ins, out.rearrange("b (c t p) f -> b c p t f", c=NC, t=TPC))
    r = _run(nc, [{f"in_{k}": v for k, v in arrays.items()}], core_ids=[0])
    return r.results[0]["out"]
```

```python
from contextlib import ExitStack

import numpy as np

import concourse.bass as bass
from concourse import mybir

F32 = mybir.dt.float32
F32R = mybir.dt.float32r
ALU = mybir.AluOpType
ACT = mybir.ActivationFunctionType
AX = mybir.AxisListType

P = 128
BATCH = 4
SEQ = 1024
CH = 512
NC = SEQ // CH
NT = SEQ // P
TPC = CH // P
E = 8
HALF = 2
UNITS = NC * E * HALF
LAG = 4
NU, NB, NX = 4, 6, 8
NP = 3
QT = 2
NQ = NT // QT
PAIRS = 5
HEADS, KV, HD = 8, 2, 32
G = HEADS // KV
ROT = HD // 4
RH = ROT // 2
NH = HEADS + KV
QKV = HEADS * HD + 2 * KV * HD
MU = G * TPC * NC
EPS = 1e-5
SCALE = float(HD) ** -0.5


def max_unit(m):
    gc, u = divmod(m, MU)
    g, qc = divmod(gc, NC)
    c, jt = divmod(u, G * TPC)
    return g, jt // TPC, qc * TPC + jt % TPC, c


def summed(k):
    return k // NT * (NT - 1) + k % NT


def unit(n):
    c, eh = divmod(n, E * HALF)
    return c, eh, slice(c * CH, (c + 1) * CH)


def woven(main, side, start, every):
    out, side = [], list(side)
    for n, step in enumerate(main):
        out.append(step)
        if n >= start and (n - start) % every == 0 and side:
            out.append(side.pop(0))
    return out + side


def recurrence_steps():
    out = []
    for k in range(2 * NC):
        out += [("gate", k), ("hidden", k), ("state", k)]
    return out + [("next_x",)] + norm_steps(0) + route_steps(0)


def norm_steps(i):
    out = []
    for c in range(NC):
        out += [("norm_turn", i, c), ("norm_apply", i, c)] + [("norm_back", i, c)] * (i < 3)
    return out


def route_steps(i):
    return [("logits", i), ("choose", i)] + [("weights", i, c) for c in range(NC)]


def first_expert_steps():
    return [("mix0", n) for n in range(UNITS + LAG)]


def second_expert_steps():
    return [("mix1", n) for n in range(UNITS + LAG)]


def project_steps():
    return norm_steps(1) + [("qkv", t) for t in range(NT)] + [("ogate", k) for k in range(KV * NC)]


def head_steps():
    turns = [[("turn_heads", q, n) for n in range(PAIRS)] for q in range(NQ)]
    maxima = [("max", m) for m in range(MU)]
    out = [("stack", 0), ("stack", 1)] + turns[0] + [("stack", 2)] + turns[1] + [("stack", 3)]
    return out + woven(turns[2] + turns[3], maxima[:MU // 2], 0, 1) + maxima[MU // 2:] + [("row", 0)]


def attention_steps():
    out, m = [], MU
    for k in range(KV * NC * NT):
        gc, t = divmod(k, NT)
        for q in range(4):
            if q % 2 == 0:
                out.append(("scores", k, q // 2))
            elif k >= 1 and q == 1:
                out.append(("values", k - 1))
            elif k >= 1:
                out.append(("sum", k - 1))
            for _ in range((2, 1, 2, 1)[q]):
                if gc < KV * NC - 1 and m < MU * (gc + 2):
                    out.append(("max", m))
                    m += 1
        if gc < KV * NC - 1 and t == NT - 2:
            out.append(("row", gc + 1))
        if gc >= 1 and t < 4:
            out.append((("take_out", "denominators", "invert", "gated")[t], gc - 1))
    last = KV * NC - 1
    return out + [("values", KV * NC * NT - 1), ("sum", KV * NC * NT - 1), ("take_out", last)]


def join_steps():
    last = KV * NC - 1
    return [("denominators", last), ("invert", last), ("gated", last)] + [("project_out", c) for c in range(NC)] \
        + norm_steps(2) + route_steps(1)


def last_norm_steps():
    return norm_steps(3) + [("store", c) for c in range(NC)]


def build_network(nc, d, out):
    ctx = ExitStack()
    place = [nc.sbuf_base]

    def sb(name, shape, dt=F32, at=None):
        size = int(np.prod(shape[1:])) * 4
        if at is None:
            place[0] = (place[0] + 31) // 32 * 32
            at, place[0] = place[0], place[0] + size
        t = nc.alloc_sbuf_tensor_at(name, shape, dt, offset=at)
        where[name] = at
        ends.append(at + size)
        return t

    with ctx:
        where, ends = {}, []

        def sem(name):
            return ctx.enter_context(nc.semaphore(name))

        ps = ctx.enter_context(nc.psum_tensor("ps", [P, 8, CH], F32))

        x_seq = sb("x_seq", [P, SEQ])
        gru_w = sb("gru_w", [P, 2, 2 * P])
        gru_b = sb("gru_b", [P, 2, 2])
        gru_hb = sb("gru_hb", [P, 2, 2])
        route_w = sb("route_w", [P, 2, E])
        route_b = sb("route_b", [P, E])
        up_w = [sb(f"up_w{i}", [P, 2, E * 2 * P], F32R) for i in range(2)]
        gate_up_w = sb("gate_up_w", [P, 2, E * 2 * P], F32R)
        down_w = [sb(f"down_w{i}", [P, 2, E * HALF * P], F32R) for i in range(2)]
        up_b = sb("up_b", [P, E * HALF])
        down_b = sb("down_b", [2 * E, P])
        qkv_w = sb("qkv_w", [P, QKV])
        ogate_w = sb("ogate_w", [P, HEADS * HD])
        out_w = sb("out_w", [P, KV, P])
        cos = sb("cos", [P, NT, RH])
        sin = sb("sin", [P, NT, RH])
        ident = sb("ident", [P, P])
        ones = sb("ones", [P, HD])
        rank = sb("rank", [P, E])
        minus_half = sb("minus_half", [P, TPC])
        pick = sb("pick", [2 * E, E], F32R)
        pick_f = sb("pick_f", [2 * E, E])

        xT = [sb(f"xT{i}", [P, SEQ]) for i in range(3)]
        xh0, xl0 = sb("xh0", [P, SEQ], F32R), sb("xl0", [P, SEQ], F32R)
        xh2, xl2 = sb("xh2", [P, SEQ], F32R), sb("xl2", [P, SEQ], F32R)
        xh, xl = {0: xh0, 2: xh2}, {0: xl0, 2: xl2}
        resid = sb("resid", [P, SEQ])
        x_tok = sb("x_tok", [P, NT, P])
        out_tok = sb("out_tok", [P, NT, P])
        g_r = sb("g_r", [P, CH], at=where["out_tok"])
        stats = sb("stats", [P, NT, 6])
        mv = sb("mv", [P, NT, 2])
        var_eps = sb("var_eps", [P, NT])
        rstd = sb("rstd", [P, NT])
        r8 = [sb(f"r8_{i}", [P, NT, E]) for i in range(6)]
        r1 = [sb(f"r1_{i}", [P, NT]) for i in range(6)]
        wstack = sb("wstack", [P, NT, 2 * E], F32R)
        wT = [sb(f"wT{i}", [2 * E, SEQ], F32R) for i in range(2)]
        mpart = sb("mpart", [P, KV, G, NT, NC])
        mneg = sb("mneg", [P, KV * NC, G * TPC])
        mrow = sb("mrow", [G * TPC, KV * NC, P], F32R)
        h_last = sb("h_last", [P, 1])
        gT = sb("gT", [P, KV, SEQ])
        rden = sb("rden", [P, TPC, G])
        dsum = sb("dsum", [P, CH])
        val = sb("val", [P, NT, KV * HD])
        qk = sb("qk", [P, NT, NH * HD])
        g_a = sb("g_a", [P, CH], at=where["qk"])
        g_z = sb("g_z", [P, CH], at=where["qk"] + 4 * CH)
        g_s = sb("g_s", [P, CH], at=where["qk"] + 8 * CH)
        hid = sb("hid", [P, SEQ], at=where["qk"] + 12 * CH)
        kT = sb("kT", [3 * HD + 1, KV, SEQ], F32R)
        region = where["kT"]
        qT = sb("qT", [3 * HD + 1, KV * NC, G, CH], F32R)
        stack = sb("stack", [P, 2, QT, NH, 3 * HD], F32R)
        rope = [sb(f"rope{i}", [P, QT, NH, RH]) for i in range(4)]
        prob = [sb(f"prob{n}", [P, G, CH], at=at)
                for n, at in enumerate((where["stack"], where["stack"] + 4 * G * CH, where["xh2"]))]
        psum = [sb(f"psum{n}", [P, 2, CH], at=where[at]) for n, at in enumerate(("xT2", "wT1"))]
        raw = sb("raw", [P, 5, E * 2 * P], at=region)
        e_t = sb("e_t", [P, CH], at=region)
        e_u = sb("e_u", [P, NU, CH], at=region + 4 * CH)
        e_h = sb("e_h", [P, NB, CH], at=region + 4 * CH * (1 + NU))
        e_hh = sb("e_hh", [P, NX, CH], F32R, at=region + 4 * CH * (1 + NU + NB))
        e_hl = sb("e_hl", [P, NX, CH], F32R, at=region + 4 * CH * (1 + NU + NB + NX))
        assert max(ends) <= nc.sbuf_usable_end, (max(ends), nc.sbuf_usable_end)

        RNN, MAXB, OB, SB0 = 4, 0, 2, 5
        DB = (3,) * (KV * NC - 1) + (7,)
        NORM_TURN = {0: 4, 1: 7, 2: 7, 3: 7}
        NORM_BACK = {0: 4, 1: 3, 2: 7}
        ROUTE = {0: 4, 1: 7}
        SPREAD, DOWN, OUTB = 4, 6, 7
        PROJ = (3, 7)
        HEADB = 2

        const_made, vec_const = sem("const_made"), sem("vec_const")
        small_in, raw_in = sem("small_in"), [sem(f"raw_in{n}") for n in range(5)]
        names = [f"norm{i}_{x}" for i in range(4) for x in ("in", "turned", "var", "rstd", "done", "back")]
        names += [f"{x}{i}_made" for i in range(3) for x in ("xh", "xT", "xl")]
        names += [f"route{i}_{x}" for i in range(2) for x in ("mm", "logit", "exp", "weight", "turned", "wT")]
        names += [f"mix{i}_{x}" for i in range(2) for x in ("mm", "act", "h", "hi", "lo", "down")]
        names += """gate_mm gate_made hidden_mm hidden_made gru_state gru_sum vec_step
            hi_made lo_made
            qkv_mm qkv_read rope_done stack_act stack_vec heads_turned headT_made
            ogate_mm ogate_done max_mm max_red max_neg mrow_turned mrow_made mrow_placed
            score_mm prob_made pv_mm pv_read pair_summed third_summed fourth_summed den_mm den_read den_turned rden_made
            rden_mm att_made wo_mm out_stored next_in ones_row""".split()
        s = {n: sem(n) for n in names}
        turn_sems = range(s[names[0]].num, s[names[-1]].num + 1)
        assert len(turn_sems) == len(names)

        raws = [("up0", up_w[0]), ("gate_up", gate_up_w), ("down0", down_w[0]),
                ("up1", up_w[1]), ("down1", down_w[1])]

        PAIR_ORDER = (PAIRS - 1,) + tuple(range(PAIRS - 1))

        def headT(pair, q):
            if pair < G * KV // 2:
                g, j = divmod(2 * pair, G)
                c, half = divmod(q, 2)
                return qT[0:3 * HD, g * NC + c, j:j + 2, half * QT * P:(half + 1) * QT * P]
            return kT[0:3 * HD, :, q * QT * P:(q + 1) * QT * P]

        def turn(steps, b=None, nxt=None):
            held = set(x for st in steps for x in (st[0], st[:2]))
            attention, experts0, experts1 = "scores" in held, "mix0" in held, "mix1" in held

            def ordinal(gc):
                return gc - 1 if gc else (KV * NC - 1 if attention else 0)

            def max_ordinal(m):
                return ordinal(m // MU) * MU + m % MU

            max_bank, before = {}, {}
            inverted = {}
            den_before = {}
            last_in, third, dens = {}, None, 0
            for name, *which in steps:
                if name == "stack":
                    third = 6
                elif name == "scores":
                    third = None if which[0] >= NT and 1 <= which[0] % NT <= 3 else 3
                elif name == "denominators":
                    den_before[which[0]], third = last_in.get(DB[which[0]], 0), None
                elif name == "gated":
                    dens += 1
                elif name == "max":
                    m = which[0]
                    max_bank[m] = min((0, 1) if third is None else (0, 1, third), key=lambda x: last_in.get(x, 0))
                    before[m] = last_in.get(max_bank[m], 0)
                    last_in[max_bank[m]] = max_ordinal(m) + 1
                    inverted[m] = dens if max_bank[m] == 3 else 0
            with nc.Block() as block:
                @block.tensor
                def _(pe):
                    def mm3(to, w, k, xhi, xlo, start=True, stop=True):
                        cols = slice(k * P, (k + 1) * P)
                        pe.matmul(to, w[:, 0, cols], xhi, start=start, stop=False)
                        pe.matmul(to, w[:, 1, cols], xhi, start=False, stop=False)
                        return pe.matmul(to, w[:, 0, cols], xlo, start=False, stop=stop)

                    def gate(k):
                        layer, c = divmod(k, NC)
                        if k == 0 and not attention:
                            pe.wait_ge(small_in, SMALL)
                            pe.wait_ge(const_made, 4)
                            pe.wait_ge(vec_const, 3)
                        if k >= 1:
                            pe.wait_ge(s["gru_state"], k)
                        x = (x_seq if layer == 0 else hid)[:, c * CH:(c + 1) * CH]
                        pe.matmul(ps[:, RNN], gru_w[:, layer, 0:P], x, start=True, stop=True)\
                          .then_inc(s["gate_mm"], 1)

                    def hidden(k):
                        layer, c = divmod(k, NC)
                        pe.wait_ge(s["gate_made"], k + 1)
                        x = (x_seq if layer == 0 else hid)[:, c * CH:(c + 1) * CH]
                        pe.matmul(ps[:, RNN], gru_w[:, layer, P:2 * P], x, start=True, stop=True)\
                          .then_inc(s["hidden_mm"], 1)

                    def norm_turn(i, c):
                        pe.wait_ge(s[f"norm{i}_in"], NC if i in (0, 2) else c + 1)
                        if c >= 1:
                            pe.wait_ge(s[f"norm{i}_done"], c)
                            if i in (0, 2):
                                pe.wait_ge(s[f"xT{i}_made"], c)
                        elif i == 1 and experts1:
                            pe.wait_ge(s["route1_wT"], NC)
                        elif i == 3 and "ogate" in held:
                            pe.wait_ge(s["ogate_done"], KV * NC)
                        for t in range(TPC):
                            tok = (c * TPC + t) * P
                            mm = pe.transpose(ps[:, NORM_TURN[i], t * P:(t + 1) * P],
                                              resid[:, tok:tok + P], ident[:])
                        mm.then_inc(s[f"norm{i}_turned"], 1)

                    def norm_back(i, c):
                        pe.wait_ge(s[f"norm{i}_done"], c + 1)
                        if c >= 1:
                            pe.wait_ge(s[f"xT{i}_made"], c)
                        for t in range(TPC):
                            mm = pe.transpose(ps[:, NORM_BACK[i], t * P:(t + 1) * P],
                                              x_tok[:, c * TPC + t], ident[:])
                        mm.then_inc(s[f"norm{i}_back"], 1)

                    def logits(i):
                        x = xT[2 * i]
                        pe.wait_ge(s[f"xT{2 * i}_made"], NC)
                        for t in range(NT):
                            mm = pe.matmul(ps[:, ROUTE[i], t * E:(t + 1) * E], x[:, t * P:(t + 1) * P],
                                           route_w[:, i], start=True, stop=True)
                        mm.then_inc(s[f"route{i}_mm"], 1)

                    def weights(i, c):
                        pe.wait_ge(s[f"route{i}_weight"], 1)
                        if c >= 1:
                            pe.wait_ge(s[f"route{i}_wT"], c)
                        for t in range(TPC):
                            mm = pe.transpose(ps[0:2 * E, ROUTE[i], t * P:(t + 1) * P],
                                              wstack[:, c * TPC + t].bitcast(F32), ident[:])
                        mm.then_inc(s[f"route{i}_turned"], 1)

                    def spread(i, n):
                        c, eh, tok = unit(n)
                        m = n // HALF
                        if m >= 2:
                            pe.wait_ge(s[f"mix{i}_h"], 2 * (m - 1))
                        pe.matmul(ps[:, SPREAD + m % 2], pick[:, eh // HALF:eh // HALF + 1].broadcast_to([2 * E, P]),
                                  wT[i][:, tok], start=True, stop=True)

                    def down(i, n):
                        c, eh, tok = unit(n)
                        if eh == 0 and c >= 1:
                            pe.wait_ge(s[f"norm{1 + 2 * i}_in"], c)
                        if eh == 0 and i == 1:
                            if c == 0 and experts0:
                                pe.wait_ge(s["norm1_in"], NC)
                            pe.matmul(ps[:, DOWN], down_b[:], wT[1][:, tok].bitcast(F32), start=True, stop=False)
                        pe.wait_ge(s[f"mix{i}_hi"], n + 1)
                        pe.wait_ge(s[f"mix{i}_lo"], n + 1)
                        mm3(ps[:, DOWN], down_w[i], eh, e_hh[:, n % NX], e_hl[:, n % NX],
                            start=i == 0 and eh == 0, stop=eh == E * HALF - 1).then_inc(s[f"mix{i}_down"], 1)

                    def mix0(n):
                        if n == 0:
                            pe.wait_ge(s["route0_wT"], NC)
                            pe.wait_ge(s["xl0_made"], NC)
                            if not attention:
                                pe.wait_ge(s["lo_made"], len(raws))
                        if n == 1 and attention:
                            pe.wait_ge(s["pv_read"], KV * NC)
                        if n < UNITS:
                            c, eh, tok = unit(n)
                            if n % HALF == 0:
                                spread(0, n)
                            if n >= 2:
                                pe.wait_ge(s["mix0_h"], n - 1)
                            mm3(ps[:, 2 * (n % 2)], up_w[0], eh, xh0[:, tok], xl0[:, tok])
                            mm3(ps[:, 2 * (n % 2) + 1], gate_up_w, eh, xh0[:, tok], xl0[:, tok])\
                                .then_inc(s["mix0_mm"], 1)
                        if n >= LAG:
                            down(0, n - LAG)

                    def mix1(n):
                        if n == 0:
                            pe.wait_ge(s["route1_wT"], NC)
                            pe.wait_ge(s["xl2_made"], NC)
                            if experts0:
                                pe.wait_ge(s["mix0_h"], UNITS)
                        if n < UNITS:
                            c, eh, tok = unit(n)
                            if n % HALF == 0:
                                spread(1, n)
                            if n >= 3:
                                pe.wait_ge(s["mix1_act"], n - 2)
                            mm3(ps[:, n % 3], up_w[1], eh, xh2[:, tok], xl2[:, tok]).then_inc(s["mix1_mm"], 1)
                        if n >= LAG:
                            down(1, n - LAG)

                    def qkv(t):
                        if t == 0:
                            pe.wait_ge(s["xT1_made"], NC)
                        if t >= 2:
                            pe.wait_ge(s["qkv_read"], t - 1)
                        pe.matmul(ps[:, PROJ[t % 2], 0:QKV], xT[1][:, t * P:(t + 1) * P], qkv_w[:],
                                  start=True, stop=True).then_inc(s["qkv_mm"], 1)

                    def ogate(k):
                        g, c = divmod(k, NC)
                        if k < 2:
                            pe.wait_ge(s["qkv_read"], NT - 1 + k)
                        else:
                            pe.wait_ge(s["ogate_done"], k - 1)
                        pe.matmul(ps[:, PROJ[k % 2]], ogate_w[:, g * P:(g + 1) * P],
                                  xT[1][:, c * CH:(c + 1) * CH], start=True, stop=True).then_inc(s["ogate_mm"], 1)

                    def turn_heads(q, turned):
                        n, pair = q * PAIRS + turned, PAIR_ORDER[turned]
                        if turned == 0:
                            pe.wait_ge(s["stack_act"], 2 * (q + 1))
                            pe.wait_ge(s["stack_vec"], q + 1)
                        if n == 0:
                            pe.wait_ge(s["ogate_done"], KV * NC)
                        if n >= 4:
                            pe.wait_ge(s["headT_made"], n - 3)
                        for j in range(2):
                            for t in range(QT):
                                mm = pe.transpose(ps[0:3 * HD, HEADB + n % 4, (j * QT + t) * P:(j * QT + t + 1) * P],
                                                  stack[:, q % 2, t, 2 * pair + j].bitcast(F32), ident[:])
                        mm.then_inc(s["heads_turned"], 1)

                    def max_(m):
                        g, j, t, c = max_unit(m)
                        n = max_ordinal(m)
                        if m == 0:
                            pe.wait_ge(s["headT_made"], NQ // NC * PAIRS)
                        if m == MU // NC:
                            pe.wait_ge(s["headT_made"], (NQ - 1) * PAIRS + 1)
                        if before[m]:
                            pe.wait_ge(s["max_red"], before[m])
                        if inverted[m]:
                            pe.wait_ge(s["att_made"], inverted[m])
                        if m % MU == 0 and ordinal(m // MU) >= 1:
                            pe.wait_ge(s["mrow_made"], ordinal(m // MU))
                        pe.matmul(ps[:, max_bank[m]], qT[0:3 * HD, g * NC + t // TPC, j, t % TPC * P:(t % TPC + 1) * P],
                                  kT[0:3 * HD, g, c * CH:(c + 1) * CH], start=True, stop=True)\
                          .then_inc(s["max_mm"], 1)

                    def row(gc):
                        pe.wait_ge(s["max_neg"], ordinal(gc) + 1)
                        pe.transpose(ps[0:G * TPC, MAXB, 0:P], mneg[:, gc], ident[:]).then_inc(s["mrow_turned"], 1)

                    def scores(k, p):
                        gc, t = divmod(k, NT)
                        if t == 0 and p == 0 and gc >= 1:
                            pe.wait_ge(s["mrow_placed"], 16 * (ordinal(gc) + 1))
                        for j in (2 * p, 2 * p + 1):
                            n = k * G + j
                            if n >= 3:
                                pe.wait_ge(s["prob_made"], n - 2)
                            pe.matmul(ps[:, SB0 + n % 3], kT[:, gc // NC, t * P:(t + 1) * P], qT[:, gc, j],
                                      start=True, stop=True).then_inc(s["score_mm"], 1)

                    def values(k):
                        gc, t = divmod(k, NT)
                        g = gc // NC
                        pe.wait_ge(s["prob_made"], G * (k + 1))
                        if t == 0 and gc >= 1:
                            pe.wait_ge(s["pv_read"], gc)
                        for j in range(G):
                            mm = pe.matmul(ps[j * HD:(j + 1) * HD, OB], val[:, t, g * HD:(g + 1) * HD],
                                           prob[k % NP][:, j], start=t == 0, stop=t == NT - 1)
                        mm.then_inc(s["pv_mm"], 1)

                    def denominators(gc):
                        for x in ("pair", "third", "fourth"):
                            pe.wait_ge(s[f"{x}_summed"], (NT - 1) * (gc + 1))
                        if gc >= 1:
                            pe.wait_ge(s["att_made"], gc)
                        if den_before[gc]:
                            pe.wait_ge(s["max_red"], den_before[gc])
                        for j in range(G):
                            mm = pe.matmul(ps[j * HD:(j + 1) * HD, DB[gc]], ones[:], psum[j // 2][:, j % 2],
                                           start=True, stop=True)
                        mm.then_inc(s["den_mm"], 1)

                    def invert(gc):
                        pe.wait_ge(s["den_read"], gc + 1)
                        for t in range(TPC):
                            mm = pe.transpose(ps[:, DB[gc], t * P:(t + 1) * P], dsum[:, t * P:(t + 1) * P], ident[:])
                        mm.then_inc(s["den_turned"], 1)

                    def gated(gc):
                        pe.wait_ge(s["rden_made"], gc + 1)
                        for t in range(TPC):
                            for j in range(G):
                                mm = pe.matmul(ps[j * HD:(j + 1) * HD, DB[gc], t * P:(t + 1) * P],
                                               rden[:, t, j:j + 1].broadcast_to([P, HD]), ident[:], start=True, stop=True)
                        mm.then_inc(s["rden_mm"], 1)

                    def project_out(c):
                        pe.wait_ge(s["att_made"], KV * NC)
                        if c >= 1:
                            pe.wait_ge(s["norm2_in"], c)
                        for g in range(KV):
                            mm = pe.matmul(ps[:, OUTB], out_w[:, g], gT[:, g, c * CH:(c + 1) * CH],
                                           start=g == 0, stop=g == KV - 1)
                        mm.then_inc(s["wo_mm"], 1)

                    own = dict(gate=gate, hidden=hidden, norm_turn=norm_turn, norm_back=norm_back, logits=logits,
                               weights=weights, mix0=mix0, mix1=mix1, qkv=qkv, ogate=ogate, turn_heads=turn_heads,
                               max=max_, row=row, scores=scores, values=values, denominators=denominators,
                               invert=invert, gated=gated, project_out=project_out)
                    for name, *which in steps:
                        if name in own:
                            own[name](*which)

                @block.scalar
                def _(act):
                    def split(n):
                        act.wait_ge(raw_in[n], 16)
                        act.activation(raws[n][1][:, 0], raw[:, n], ACT.Copy).then_inc(s["hi_made"], 1)

                    def gate(k):
                        layer = k // NC
                        act.wait_ge(s["gate_mm"], k + 1)
                        act.activation(g_z[:], ps[:, RNN], ACT.Tanh, scale=0.5, bias=gru_hb[:, layer, 0:1])\
                           .then_inc(s["gate_made"], 1)

                    def hidden(k):
                        layer = k // NC
                        act.wait_ge(s["hidden_mm"], k + 1)
                        act.activation(g_s[:], ps[:, RNN], ACT.Tanh, scale=0.5, bias=gru_hb[:, layer, 1:2])\
                           .then_inc(s["hidden_made"], 1)

                    def norm_back(i, c):
                        tok = slice(c * CH, (c + 1) * CH)
                        act.wait_ge(s[f"norm{i}_back"], c + 1)
                        if i != 1:
                            act.activation(xh[i][:, tok], ps[:, NORM_BACK[i]], ACT.Copy).then_inc(s[f"xh{i}_made"], 1)
                        act.activation(xT[i][:, tok], ps[:, NORM_BACK[i]], ACT.Copy).then_inc(s[f"xT{i}_made"], 1)

                    def choose(i):
                        act.wait_ge(s[f"route{i}_logit"], 1)
                        act.activation(r8[1][:], r8[0][:], ACT.Exp).then_inc(s[f"route{i}_exp"], 1)

                    def weights(i, c):
                        act.wait_ge(s[f"route{i}_turned"], c + 1)
                        act.activation(wT[i][:, c * CH:(c + 1) * CH], ps[0:2 * E, ROUTE[i]], ACT.Copy)\
                           .then_inc(s[f"route{i}_wT"], 1)

                    def hi(i, n):
                        act.wait_ge(s[f"mix{i}_h"], n + 1)
                        if n >= NX:
                            act.wait_ge(s[f"mix{i}_down"], n - NX + 1)
                        act.activation(e_hh[:, n % NX], e_h[:, n % NB], ACT.Copy).then_inc(s[f"mix{i}_hi"], 1)

                    def mix0(n):
                        if n < UNITS:
                            act.wait_ge(s["mix0_mm"], n + 1)
                            if n >= NU:
                                act.wait_ge(s["mix0_h"], n - NU + 1)
                            act.activation(e_u[:, n % NU], ps[:, 2 * (n % 2)], ACT.Silu).then_inc(s["mix0_act"], 1)
                        if 1 <= n <= UNITS:
                            hi(0, n - 1)

                    def mix1(n):
                        if n == 0 and experts0:
                            act.wait_ge(s["mix0_down"], UNITS)
                        if n < UNITS:
                            eh = n % (E * HALF)
                            act.wait_ge(s["mix1_mm"], n + 1)
                            if n >= NU:
                                act.wait_ge(s["mix1_h"], n - NU + 1)
                            act.activation(e_u[:, n % NU], ps[:, n % 3], ACT.Relu, bias=up_b[:, eh:eh + 1])\
                               .then_inc(s["mix1_act"], 1)
                        if 1 <= n <= UNITS:
                            hi(1, n - 1)

                    def qkv(t):
                        act.wait_ge(s["qkv_mm"], t + 1)
                        act.activation(qk[:, t], ps[:, PROJ[t % 2], 0:NH * HD], ACT.Copy)
                        act.activation(val[:, t], ps[:, PROJ[t % 2], NH * HD:QKV], ACT.Copy).then_inc(s["qkv_read"], 1)

                    def ogate(k):
                        g, c = divmod(k, NC)
                        act.wait_ge(s["ogate_mm"], k + 1)
                        act.activation(gT[:, g, c * CH:(c + 1) * CH], ps[:, PROJ[k % 2]], ACT.Silu)\
                           .then_inc(s["ogate_done"], 1)

                    def stack_(q):
                        if q == 0:
                            act.wait_ge(s["mix1_down" if experts1 else "mix0_down"], UNITS)
                        act.wait_ge(s["rope_done"], q + 1)
                        if q >= 2:
                            act.wait_ge(s["heads_turned"], PAIRS * (q - 1))
                        x = qk[:, q * QT:(q + 1) * QT].rearrange("p t (h f) -> p t h f", f=HD)
                        act.activation(stack[:, q % 2, :, :, 0:HD], x, ACT.Copy).then_inc(s["stack_act"], 1)
                        act.activation(stack[:, q % 2, :, 0:HEADS, 2 * HD:3 * HD], x[:, :, 0:HEADS], ACT.Copy)
                        act.activation(stack[:, q % 2, :, HEADS:NH, HD:2 * HD], x[:, :, HEADS:NH], ACT.Copy)\
                           .then_inc(s["stack_act"], 1)

                    def turn_heads(q, turned):
                        n = q * PAIRS + turned
                        act.wait_ge(s["heads_turned"], n + 1)
                        got = ps[0:3 * HD, HEADB + n % 4].rearrange("p (j t) -> p j t", j=2)
                        act.activation(headT(PAIR_ORDER[turned], q), got, ACT.Copy).then_inc(s["headT_made"], 1)

                    def scores(k, p):
                        for j in (2 * p, 2 * p + 1):
                            act.wait_ge(s["score_mm"], k * G + j + 1)
                            if k >= NP:
                                act.wait_ge(s["pv_mm"], k - NP + 1)
                                act.wait_ge(s[("pair_summed", "pair_summed", "third_summed", "fourth_summed")[j]],
                                            summed(k - NP) + ((k - NP) % NT == 0))
                            act.activation(prob[k % NP][:, j], ps[:, SB0 + (k * G + j) % 3], ACT.Exp, scale=SCALE)\
                               .then_inc(s["prob_made"], 1)

                    def denominators(gc):
                        act.wait_ge(s["den_mm"], gc + 1)
                        if gc >= 1:
                            act.wait_ge(s["den_turned"], gc)
                        act.activation(dsum[:], ps[:, DB[gc]], ACT.Copy).then_inc(s["den_read"], 1)

                    own = dict(split=split, gate=gate, hidden=hidden, norm_back=norm_back, choose=choose,
                               weights=weights, mix0=mix0, mix1=mix1, qkv=qkv, ogate=ogate, stack=stack_,
                               turn_heads=turn_heads, scores=scores, denominators=denominators)
                    for name, *which in steps:
                        if name in own:
                            own[name](*which)

                @block.vector
                def _(vec):
                    chain = [0]

                    def then(ins):
                        chain[0] += 1
                        ins.then_inc(s["vec_step"], 1)
                        vec.wait_ge(s["vec_step"], chain[0])

                    def split(n):
                        vec.wait_ge(s["hi_made"], n + 1)
                        w = raws[n][1]
                        vec.tensor_tensor(w[:, 1], raw[:, n], w[:, 0].bitcast(F32), ALU.subtract)\
                           .then_inc(s["lo_made"], 1)

                    def state(k):
                        layer, c = divmod(k, NC)
                        vec.wait_ge(s["gate_made"], k + 1)
                        vec.tensor_scalar(g_a[:], g_z[:], -0.5, 0.5, ALU.mult, ALU.add)
                        vec.wait_ge(s["hidden_made"], k + 1)
                        vec.tensor_scalar(g_r[:], ps[:, RNN], gru_b[:, layer, 1:2], 0.0, ALU.add, ALU.max)
                        then(vec.tensor_scalar(g_s[:], g_s[:], 0.0, 0.5, ALU.min, ALU.mult))
                        then(vec.scalar_tensor_tensor(g_s[:], g_s[:], 0.5, g_r[:], ALU.add, ALU.add))
                        then(vec.scalar_tensor_tensor(g_z[:], g_z[:], 1.0, g_s[:], ALU.add, ALU.mult))
                        to = (hid if layer == 0 else resid)[:, c * CH:(c + 1) * CH]
                        first = 1.0 if c == 0 else hid[:, c * CH - 1:c * CH] if layer == 0 else h_last[:]
                        vec.tensor_tensor_scan(to, g_a[:], g_z[:], first, ALU.mult, ALU.add)\
                           .then_inc(s["gru_state"], 1)
                        vec.wait_ge(s["gru_state"], k + 1)
                        if layer == 1:
                            if c == 0:
                                then(vec.tensor_copy(h_last[:], to[:, CH - 1:CH]))
                            vec.scalar_tensor_tensor(to, to, 0.5, x_seq[:, c * CH:(c + 1) * CH], ALU.mult, ALU.add)\
                               .then_inc(s["norm0_in"], 1)

                    def norm_turn(i, c):
                        vec.wait_ge(s[f"norm{i}_turned"], c + 1)
                        tile = [ps[:, NORM_TURN[i], t * P:(t + 1) * P] for t in range(TPC)]
                        ts = range(TPC * c, TPC * (c + 1))
                        cs = slice(TPC * c, TPC * (c + 1))
                        for t in ts:
                            last = vec.bn_stats(stats[:, t], tile[t % TPC])
                        then(last)
                        for t in ts:
                            last = vec.bn_aggr(mv[:, t], stats[:, t])
                        then(last)
                        vec.tensor_scalar(var_eps[:, cs], mv[:, cs, 1], EPS, None, ALU.add)\
                           .then_inc(s[f"norm{i}_var"], 1)

                    def norm_apply(i, c):
                        vec.wait_ge(s[f"norm{i}_rstd"], c + 1)
                        tile = [ps[:, NORM_TURN[i], t * P:(t + 1) * P] for t in range(TPC)]
                        to = out_tok if i == 3 else x_tok
                        for t in range(TPC * c, TPC * (c + 1)):
                            last = vec.tensor_scalar(to[:, t], tile[t % TPC], mv[:, t, 0:1], rstd[:, t:t + 1],
                                                     ALU.subtract, ALU.mult)
                        last.then_inc(s[f"norm{i}_done"], 1)

                    def norm_back(i, c):
                        if i == 1:
                            return
                        tok = slice(c * CH, (c + 1) * CH)
                        vec.wait_ge(s[f"xT{i}_made"], c + 1)
                        vec.tensor_tensor(xl[i][:, tok], xT[i][:, tok], xh[i][:, tok].bitcast(F32), ALU.subtract)\
                           .then_inc(s[f"xl{i}_made"], 1)

                    def over(x):
                        return x.rearrange("p (t e) -> p t e", e=1).broadcast_to([P, NT, E])

                    def logits(i):
                        lg, pr, mx = r8[0][:], r8[2][:], r1[0][:]
                        vec.wait_ge(s[f"route{i}_mm"], 1)
                        got = ps[:, ROUTE[i], 0:NT * E].rearrange("p (t e) -> p t e", e=E)
                        if i == 0:
                            then(vec.tensor_copy(pr, got))
                        else:
                            bias = route_b[:].rearrange("p (t e) -> p t e", t=1).broadcast_to([P, NT, E])
                            then(vec.tensor_tensor(pr, got, bias, ALU.add))
                        then(vec.tensor_reduce(mx, pr, AX.X, ALU.max))
                        vec.tensor_tensor(lg, pr, over(mx), ALU.subtract).then_inc(s[f"route{i}_logit"], 1)

                    def choose(i):
                        ex, pr, eq, oh1, oh2 = (r[:] for r in r8[1:])
                        sm, m1, v, m2, tmp = (r[:] for r in r1[1:])
                        vec.wait_ge(s[f"route{i}_exp"], 1)
                        then(vec.tensor_reduce(sm, ex, AX.X, ALU.add))
                        then(vec.reciprocal(tmp, sm))
                        then(vec.tensor_tensor(pr, ex, over(tmp), ALU.mult))
                        ranks = rank[:].rearrange("p (t e) -> p t e", t=1).broadcast_to([P, NT, E])

                        def first_of(x, m, oh):
                            then(vec.tensor_reduce(m, x, AX.X, ALU.max))
                            then(vec.tensor_tensor(eq, x, over(m), ALU.is_equal))
                            then(vec.tensor_tensor(eq, eq, ranks, ALU.mult))
                            then(vec.tensor_reduce(v, eq, AX.X, ALU.max))
                            then(vec.tensor_tensor(oh, eq, over(v), ALU.is_equal))

                        first_of(pr, m1, oh1)
                        then(vec.scalar_tensor_tensor(ex, oh1, -2.0, pr, ALU.mult, ALU.add))
                        first_of(ex, m2, oh2)
                        then(vec.tensor_tensor(oh1, oh1, oh2, ALU.add))
                        then(vec.tensor_tensor(pr, pr, oh1, ALU.mult))
                        if i == 0:
                            then(vec.tensor_tensor(sm, m1, m2, ALU.add))
                            then(vec.reciprocal(tmp, sm))
                            then(vec.tensor_tensor(pr, pr, over(tmp), ALU.mult))
                        elif ("logits", 0) in held:
                            vec.wait_ge(s["route0_turned"], NC)
                        then(vec.tensor_copy(wstack[:, :, 0:E], pr))
                        vec.tensor_tensor(wstack[:, :, E:2 * E], pr, wstack[:, :, 0:E].bitcast(F32),
                                          ALU.subtract).then_inc(s[f"route{i}_weight"], 1)

                    def add_down(i, n):
                        c, eh, tok = unit(n)
                        if eh == E * HALF - 1:
                            if i == 0 and ("norm_turn", 2) in held:
                                vec.wait_ge(s["norm2_turned"], NC)
                            if i == 1 and ("norm_turn", 1) in held:
                                vec.wait_ge(s["norm1_turned"], NC)
                            vec.wait_ge(s[f"mix{i}_down"], n + 1)
                            vec.tensor_tensor(resid[:, tok], xT[2 * i][:, tok], ps[:, DOWN], ALU.add)\
                               .then_inc(s[f"norm{1 + 2 * i}_in"], 1)

                    def mix0(n):
                        if n < UNITS:
                            vec.wait_ge(s["mix0_act"], n + 1)
                            then(vec.tensor_tensor(e_t[:], e_u[:, n % NU], ps[:, SPREAD + n // HALF % 2], ALU.mult))
                            if n >= NB:
                                vec.wait_ge(s["mix0_lo"], n - NB + 1)
                            vec.tensor_tensor(e_h[:, n % NB], e_t[:], ps[:, 2 * (n % 2) + 1], ALU.mult)\
                               .then_inc(s["mix0_h"], 1)
                            vec.wait_ge(s["mix0_h"], n + 1)
                        if n >= LAG:
                            add_down(0, n - LAG)

                    def mix1(n):
                        if n == 0 and experts0:
                            vec.wait_ge(s["mix0_lo"], UNITS)
                        if n < UNITS:
                            vec.wait_ge(s["mix1_act"], n + 1)
                            if n >= NB:
                                vec.wait_ge(s["mix1_lo"], n - NB + 1)
                            vec.tensor_tensor(e_h[:, n % NB], e_u[:, n % NU], ps[:, SPREAD + n // HALF % 2], ALU.mult)\
                               .then_inc(s["mix1_h"], 1)
                        if n >= LAG:
                            add_down(1, n - LAG)

                    def stack_(q):
                        cs = slice(q * QT, (q + 1) * QT)
                        vec.wait_ge(s["qkv_read"], QT * (q + 1))
                        if q == 0:
                            vec.wait_ge(s["mix1_down" if experts1 else "mix0_down"], UNITS)
                        if q >= 2:
                            vec.wait_ge(s["heads_turned"], PAIRS * (q - 1))
                        x = qk[:, cs].rearrange("p t (h f) -> p t h f", f=HD)
                        x1, x2 = x[:, :, :, 0:RH], x[:, :, :, RH:ROT]
                        co, si = (w[:, cs].rearrange("p t (h f) -> p t h f", h=1)
                                  .broadcast_to([P, QT, NH, RH]) for w in (cos, sin))
                        x1c, x2s, x2c, x1s = (r[:] for r in rope)
                        vec.tensor_tensor(x1c, x1, co, ALU.mult)
                        vec.tensor_tensor(x2s, x2, si, ALU.mult)
                        vec.tensor_tensor(x2c, x2, co, ALU.mult)
                        then(vec.tensor_tensor(x1s, x1, si, ALU.mult))
                        vec.tensor_tensor(x1, x1c, x2s, ALU.subtract)
                        vec.tensor_tensor(x2, x2c, x1s, ALU.add).then_inc(s["rope_done"], 1)
                        vec.wait_ge(s["rope_done"], q + 1)
                        vec.wait_ge(s["stack_act"], 2 * q + 1)
                        to = stack[:, q % 2]
                        qs, ks = slice(0, HEADS), slice(HEADS, NH)
                        hi = to[:, :, :, 0:HD].bitcast(F32)
                        vec.tensor_tensor(to[:, :, qs, HD:2 * HD], x[:, :, qs], hi[:, :, qs], ALU.subtract)
                        vec.tensor_tensor(to[:, :, ks, 2 * HD:3 * HD], x[:, :, ks], hi[:, :, ks], ALU.subtract)\
                           .then_inc(s["stack_vec"], 1)

                    def max_(m):
                        g, j, t, c = max_unit(m)
                        vec.wait_ge(s["max_mm"], max_ordinal(m) + 1)
                        vec.tensor_reduce(mpart[:, g, j, t, c:c + 1], ps[:, max_bank[m]], AX.X, ALU.max)\
                           .then_inc(s["max_red"], 1)

                    def row(gc):
                        n = ordinal(gc)
                        vec.wait_ge(s["max_red"], (n + 1) * MU)
                        vec.tensor_reduce(mneg[:, gc].rearrange("p (j t) -> p j t", j=G),
                                          mpart[:, gc // NC, :, gc % NC * TPC:(gc % NC + 1) * TPC],
                                          AX.X, ALU.max, negate=True).then_inc(s["max_neg"], 1)
                        vec.wait_ge(s["mrow_turned"], n + 1)
                        vec.tensor_copy(mrow[:, gc], ps[0:G * TPC, MAXB, 0:P]).then_inc(s["mrow_made"], 1)

                    def sum_(k):
                        gc, t = divmod(k, NT)
                        if t == 0:
                            return
                        vec.wait_ge(s["prob_made"], G * (k + 1))
                        if t == 1 and gc >= 1:
                            vec.wait_ge(s["den_mm"], gc)
                        if t >= 2:
                            vec.wait_ge(s["fourth_summed"], summed(k) - 1)
                        to = psum[1][:, 1]
                        vec.tensor_tensor(to, to if t >= 2 else prob[(k - 1) % NP][:, 3], prob[k % NP][:, 3], ALU.add)\
                           .then_inc(s["fourth_summed"], 1)

                    def take_out(gc):
                        g, c = divmod(gc, NC)
                        to = gT[:, g, c * CH:(c + 1) * CH]
                        vec.wait_ge(s["pv_mm"], NT * (gc + 1))
                        vec.tensor_tensor(to, to, ps[:, OB], ALU.mult).then_inc(s["pv_read"], 1)

                    def invert(gc):
                        vec.wait_ge(s["den_turned"], gc + 1)
                        one_of_head = ps[:, DB[gc]].rearrange("p (t j f) -> p t j f", t=TPC, j=G)[:, :, :, 0]
                        vec.reciprocal(rden[:], one_of_head).then_inc(s["rden_made"], 1)

                    def gated(gc):
                        g, c = divmod(gc, NC)
                        to = gT[:, g, c * CH:(c + 1) * CH]
                        vec.wait_ge(s["rden_mm"], gc + 1)
                        vec.wait_ge(s["pv_read"], gc + 1)
                        vec.tensor_tensor(to, to, ps[:, DB[gc]], ALU.mult).then_inc(s["att_made"], 1)

                    def project_out(c):
                        tok = slice(c * CH, (c + 1) * CH)
                        vec.wait_ge(s["wo_mm"], c + 1)
                        vec.tensor_tensor(resid[:, tok], xT[1][:, tok], ps[:, OUTB], ALU.add)\
                           .then_inc(s["norm2_in"], 1)

                    own = dict(split=split, state=state, norm_turn=norm_turn, norm_apply=norm_apply,
                               norm_back=norm_back, logits=logits, choose=choose, mix0=mix0, mix1=mix1, stack=stack_,
                               max=max_, row=row, sum=sum_, take_out=take_out, invert=invert,
                               gated=gated, project_out=project_out)
                    for name, *which in steps:
                        if name in own:
                            own[name](*which)

                @block.gpsimd
                def _(pool):
                    def norm_turn(i, c):
                        cs = slice(TPC * c, TPC * (c + 1))
                        pool.wait_ge(s[f"norm{i}_var"], c + 1)
                        pool.tensor_tensor(rstd[:, cs], var_eps[:, cs], minus_half[:], ALU.pow)\
                            .then_inc(s[f"norm{i}_rstd"], 1)

                    def sum_(k):
                        gc, t = divmod(k, NT)
                        if t == 0:
                            return
                        if t == 1 and gc >= 1:
                            pool.wait_ge(s["den_mm"], gc)
                        for name, heads, to in (("pair", slice(0, 2), psum[0][:]), ("third", slice(2, 3), psum[1][:, 0:1])):
                            pool.wait_ge(s["prob_made"], G * k + heads.stop)
                            if t >= 2:
                                pool.wait_ge(s[f"{name}_summed"], summed(k) - 1)
                            pool.tensor_tensor(to, to if t >= 2 else prob[(k - 1) % NP][:, heads],
                                               prob[k % NP][:, heads], ALU.add).then_inc(s[f"{name}_summed"], 1)

                    def lo(i, n):
                        pool.wait_ge(s[f"mix{i}_hi"], n + 1)
                        if n >= NX:
                            pool.wait_ge(s[f"mix{i}_down"], n - NX + 1)
                        pool.tensor_tensor(e_hl[:, n % NX], e_h[:, n % NB], e_hh[:, n % NX].bitcast(F32),
                                           ALU.subtract).then_inc(s[f"mix{i}_lo"], 1)

                    def mix0(n):
                        if 1 <= n <= UNITS:
                            lo(0, n - 1)

                    def mix1(n):
                        if n == 1 and experts0:
                            pool.wait_ge(s["mix0_down"], UNITS)
                        if 1 <= n <= UNITS:
                            lo(1, n - 1)

                    def stack_(q):
                        if q == 0:
                            pool.wait_ge(s["mix1_down" if experts1 else "mix0_down"], UNITS)
                            pool.wait_ge(s["norm1_rstd"], NC)
                            pool.memset(kT[3 * HD:3 * HD + 1].bitcast(F32), 1.0).then_inc(s["ones_row"], 1)
                            pool.wait_ge(s["ones_row"], 1)

                    own = dict(norm_turn=norm_turn, mix0=mix0, mix1=mix1, stack=stack_, sum=sum_)
                    for name, *which in steps:
                        if name in own:
                            own[name](*which)

                @block.sync
                def _(sp):
                    def next_x():
                        sp.wait_ge(s["norm0_in"], NC)
                        sp.dma_start(x_seq[:], d["xT"][nxt]).then_inc(s["next_in"], 16)

                    def row(gc):
                        sp.wait_ge(s["mrow_made"], ordinal(gc) + 1)
                        sp.dma_start(qT[3 * HD:3 * HD + 1, gc].bitcast(F32), mrow[:, gc].bitcast(F32))\
                          .then_inc(s["mrow_placed"], 16)

                    def store(c):
                        sp.wait_ge(s["norm3_done"], c + 1)
                        sp.dma_start(out[b, c], out_tok[:, c * TPC:(c + 1) * TPC]).then_inc(s["out_stored"], 16)

                    own = dict(next_x=next_x, row=row, store=store)
                    for name, *which in steps:
                        if name in own:
                            own[name](*which)
                    rows = sum(st[0] == "row" for st in steps)
                    sp.wait_ge(s["mrow_placed"], 16 * rows)
                    if ("store", 0) in steps:
                        sp.wait_ge(s["out_stored"], 16 * NC)
                    if ("next_x",) in steps:
                        sp.wait_ge(s["next_in"], 16)

        def clear():
            with nc.Block() as block:
                @block.sync
                def _(sp):
                    sp.sem_clear(turn_sems)

        small = [(x_seq[:], d["xT"][0]), (gru_w[:], d["gru_w"]), (gru_b[:], d["gru_b"]), (route_w[:], d["route_w"]),
                 (route_b[:], d["route_b"]), (up_b[:], d["up_b"]), (down_b[:], d["down_b"]),
                 (qkv_w[:], d["qkv_w"]), (ogate_w[:], d["ogate_w"]), (out_w[:], d["out_w"]),
                 (cos[:], d["cos"]), (sin[:], d["sin"])]
        SMALL = 16 * len(small)

        with nc.Block() as block:
            @block.sync
            def _(sp):
                for to, of in small:
                    sp.dma_start(to, of).then_inc(small_in, 16)
                for n in range(0, len(raws)):
                    sp.dma_start(raw[:, n], d[raws[n][0]]).then_inc(raw_in[n], 16)

            @block.vector
            def _(vec):
                vec.memset(ones[:], 1.0)
                vec.memset(minus_half[:], -0.5)
                for e in range(E):
                    last = vec.memset(rank[:, e:e + 1], float(E - e))
                last.then_inc(vec_const, 1)
                vec.wait_ge(const_made, 4)
                vec.tensor_copy(pick[:], pick_f[:]).then_inc(vec_const, 1)
                vec.wait_ge(small_in, SMALL)
                vec.tensor_scalar(gru_hb[:], gru_b[:], 0.5, None, ALU.mult)
                vec.tensor_scalar(gru_w[:, 1], gru_w[:, 1], 0.5, None, ALU.mult).then_inc(vec_const, 1)

            @block.gpsimd
            def _(pool):
                pool.memset(ident[:], 0.0).then_inc(const_made, 1)
                pool.memset(pick_f[:], 0.0).then_inc(const_made, 1)
                pool.wait_ge(const_made, 2)
                pool.affine_select(out=ident[:], in_=ident[:], compare_op=ALU.not_equal, fill=1.0,
                                   base=0, pattern=[[-1, P]], channel_multiplier=1)
                pool.affine_select(out=pick_f[:], in_=pick_f[:], compare_op=ALU.not_equal, fill=1.0,
                                   base=0, pattern=[[-1, E]], channel_multiplier=1).then_inc(const_made, 1)
                pool.wait_ge(const_made, 3)
                pool.affine_select(out=pick_f[:], in_=pick_f[:], compare_op=ALU.not_equal, fill=1.0,
                                   base=-E, pattern=[[-1, E]], channel_multiplier=1).then_inc(const_made, 1)

        splits = [("split", n) for n in range(len(raws))]
        side = woven(recurrence_steps(), splits, 2, 2)
        turn(side + first_expert_steps() + project_steps() + head_steps(), nxt=1)
        clear()
        beside_c = woven(attention_steps(), recurrence_steps(), 24, 8)
        beside_d = woven(first_expert_steps(), join_steps(), 2, 2)
        beside_e = woven(second_expert_steps(), project_steps(), 0, 2)
        beside_h = woven(head_steps(), last_norm_steps(), 3, 3)
        with nc.Fori(0, BATCH - 1) as b:
            turn(beside_c + beside_d + beside_e + beside_h, b=b, nxt=(b + 2) % BATCH)
            clear()
        turn(attention_steps() + join_steps() + second_expert_steps() + last_norm_steps(), b=BATCH - 1)


def rotary_table():
    inv = (1.0 / np.float32(10000.0) ** (np.arange(0, ROT, 2, dtype=np.float32) / np.float32(ROT)))
    freqs = np.arange(SEQ, dtype=np.float32)[:, None] * inv.astype(np.float32)[None, :]
    split = lambda a: np.ascontiguousarray(a.astype(np.float32).reshape(NT, P, RH).transpose(1, 0, 2))
    return split(np.cos(freqs)), split(np.sin(freqs))


def lay_out(a):
    t = np.ascontiguousarray
    cos, sin = rotary_table()
    by_partition = lambda w: t(w.reshape(-1, HALF, P, P).transpose(2, 0, 1, 3).reshape(P, -1))
    wq, wk, wv = a["L1_attn_Wq"], a["L1_attn_Wk"], a["L1_attn_Wv"]
    return {
        "xT": t(a["L0_attn_x"].transpose(0, 2, 1)),
        "gru_w": t(np.stack([a["L0_attn_W0"].T, a["L0_attn_W1"].T], 1)),
        "gru_b": t(np.stack([a["L0_attn_b0"].reshape(2, P).T, a["L0_attn_b1"].reshape(2, P).T], 1)),
        "route_w": t(np.stack([a["L0_ffn_wg"].T, a["L1_ffn_gate_w"].T], 1)),
        "route_b": t(np.repeat(a["L1_ffn_gate_b"][None], P, 0)),
        "up0": t(a["L0_ffn_w1"].transpose(2, 0, 1).reshape(P, -1)),
        "gate_up": t(a["L0_ffn_w3"].transpose(2, 0, 1).reshape(P, -1)),
        "down0": by_partition(a["L0_ffn_w2"].transpose(0, 2, 1)),
        "up1": t(a["L1_ffn_w1"].transpose(1, 0, 2).reshape(P, -1)),
        "down1": by_partition(a["L1_ffn_w2"]),
        "up_b": t(a["L1_ffn_b1"].reshape(E * HALF, P).T),
        "down_b": t(np.concatenate([a["L1_ffn_b2"]] * 2, 0)),
        "qkv_w": t(np.concatenate([wq[:, :HEADS * HD], wk, wv], 1)),
        "ogate_w": t(wq[:, HEADS * HD:]),
        "out_w": t(a["L1_attn_Wo"].reshape(KV, P, P).transpose(1, 0, 2)),
        "cos": cos,
        "sin": sin,
    }


def kernel(**inputs):
    import concourse.bacc as _bacc
    from concourse.bass_utils import run_bass_kernel_spmd as _run

    arrays = lay_out({k: np.asarray(v) for k, v in inputs.items()})
    nc = _bacc.Bacc("TRN2", target_bir_lowering=False, num_devices=1, dynamic_dma_scratch_size=1024)
    ins = {k: nc.dram_tensor(f"in_{k}", v.shape, mybir.dt.from_np(v.dtype), kind="ExternalInput").ap()
           for k, v in arrays.items()}
    out = nc.dram_tensor("out", (BATCH, SEQ, P), F32, kind="ExternalOutput").ap()
    build_network(nc, ins, out.rearrange("b (c t p) f -> b c p t f", c=NC, t=TPC))
    r = _run(nc, [{f"in_{k}": v for k, v in arrays.items()}], core_ids=[0])
    return r.results[0]["out"]
```

```python
from contextlib import ExitStack

import numpy as np

import concourse.bass as bass
from concourse import mybir

F32 = mybir.dt.float32
F32R = mybir.dt.float32r
ALU = mybir.AluOpType
ACT = mybir.ActivationFunctionType
AX = mybir.AxisListType

P = 128
BATCH = 4
SEQ = 1024
CH = 512
NC = SEQ // CH
NT = SEQ // P
TPC = CH // P
E = 8
HALF = 2
UNITS = NC * E * HALF
LAG = 4
NU, NB, NX = 4, 6, 8
NP = 3
QT = 2
NQ = NT // QT
PAIRS = 5
HEADS, KV, HD = 8, 2, 32
G = HEADS // KV
ROT = HD // 4
RH = ROT // 2
NH = HEADS + KV
QKV = HEADS * HD + 2 * KV * HD
MU = G * TPC * NC
EPS = 1e-5
SCALE = float(HD) ** -0.5


PROJ_OPS = TPC + KV


def group_and_chunk(gc):
    c, g = divmod(gc, KV)
    return g, c


def max_unit(m):
    gc, u = divmod(m, MU)
    g, qc = group_and_chunk(gc)
    c, jt = divmod(u, G * TPC)
    return g, jt // TPC, qc * TPC + jt % TPC, c


def summed(k):
    return k // NT * (NT - 1) + k % NT


def unit(n):
    c, eh = divmod(n, E * HALF)
    return c, eh, slice(c * CH, (c + 1) * CH)


def woven(main, side, start, every, close=1):
    out, side, due = [], list(side), start
    for n, step in enumerate(main):
        out.append(step)
        if n >= due and side:
            out.append(side.pop(0))
            goes_on = side and side[0][0] in ("state", "choose") and side[0][-1] > 0
            due = n + (close if goes_on else every)
    return out + side


def recurrence_steps(c):
    out = []
    for k in (2 * c, 2 * c + 1):
        out += [("gate", k), ("hidden", k)] + [("state", k, part) for part in range(4 + k % 2)]
    return out + [("next_x",)] * (c == NC - 1)


def norm_steps(i, c):
    return [("norm_turn", i, c), ("norm_apply", i, c)] + [("norm_back", i, c)] * (i < 3)


def route_steps(i, c, n=1):
    return [("logits", i, c, n)] + [("choose", i, c, n, part) for part in range(5)] \
        + [("weights", i, k) for k in range(c, c + n)]


def first_expert_steps():
    return [("mix0", n) for n in range(UNITS + LAG)]


def second_expert_steps():
    return [("mix1", n) for n in range(UNITS + LAG)]


def project_steps(c):
    return norm_steps(1, c) + [("qkv", t) for t in range(c * TPC, (c + 1) * TPC)] \
        + [("ogate", g, c) for g in range(KV)] \
        + [("rope", q) for q in range(c * NQ // NC, (c + 1) * NQ // NC)]


def head_steps():
    turns = [[("turn_heads", q, n) for n in range(PAIRS)] for q in range(NQ)]
    maxima = [("max", m) for m in range(MU)]
    out = [("stack", 0), ("stack", 1)] + turns[0] + [("stack", 2)] + turns[1] + [("stack", 3)]
    return out + woven(turns[2] + turns[3], maxima[:MU // 2], 0, 1) + maxima[MU // 2:] + [("row", 0)]


def attention_steps():
    out, m = [], MU
    for k in range(KV * NC * NT):
        gc, t = divmod(k, NT)
        for q in range(4):
            if q % 2 == 0:
                out.append(("scores", k, q // 2))
            elif k >= 1 and q == 1:
                out.append(("values", k - 1))
            elif k >= 1:
                out.append(("sum", k - 1))
            for _ in range((2, 1, 1, 1)[q]):
                if gc < KV * NC - 1 and m < MU * (gc + 2):
                    out.append(("max", m))
                    m += 1
        if gc < KV * NC - 1 and t == NT - 2:
            out.append(("row", gc + 1))
        if gc >= 1 and t < 4:
            out.append((("take_out", "denominators", "invert", "gated")[t], gc - 1))
    last = KV * NC - 1
    return out + [("values", KV * NC * NT - 1), ("sum", KV * NC * NT - 1), ("take_out", last)]


def last_part_steps():
    last = KV * NC - 1
    return [(name, last) for name in ("denominators", "invert", "gated")]


def last_norm_steps():
    return norm_steps(3, 0) + norm_steps(3, 1) + [("store", c) for c in range(NC)]


def build_network(nc, d, out):
    ctx = ExitStack()
    place = [nc.sbuf_base]

    def sb(name, shape, dt=F32, at=None):
        size = int(np.prod(shape[1:])) * 4
        if at is None:
            place[0] = (place[0] + 31) // 32 * 32
            at, place[0] = place[0], place[0] + size
        t = nc.alloc_sbuf_tensor_at(name, shape, dt, offset=at)
        where[name] = at
        ends.append(at + size)
        return t

    with ctx:
        where, ends = {}, []

        def sem(name):
            return ctx.enter_context(nc.semaphore(name))

        ps = ctx.enter_context(nc.psum_tensor("ps", [P, 8, CH], F32))

        x_seq = sb("x_seq", [P, SEQ])
        gru_w = sb("gru_w", [P, 2, 2 * P])
        gru_b = sb("gru_b", [P, 2, 2])
        gru_hb = sb("gru_hb", [P, 2, 2])
        route_w = sb("route_w", [P, 2, E])
        route_b = sb("route_b", [P, E])
        up_w = [sb(f"up_w{i}", [P, 2, E * 2 * P], F32R) for i in range(2)]
        gate_up_w = sb("gate_up_w", [P, 2, E * 2 * P], F32R)
        down_w = [sb(f"down_w{i}", [P, 2, E * HALF * P], F32R) for i in range(2)]
        up_b = sb("up_b", [P, E * HALF])
        down_b = sb("down_b", [2 * E, P])
        qkv_w = sb("qkv_w", [P, QKV])
        ogate_w = sb("ogate_w", [P, HEADS * HD])
        out_w = sb("out_w", [P, KV, P])
        cos = sb("cos", [P, NT, RH])
        sin = sb("sin", [P, NT, RH])
        ident = sb("ident", [P, P])
        ones = sb("ones", [P, HD])
        rank = sb("rank", [P, E])
        minus_half = sb("minus_half", [P, TPC])
        pick = sb("pick", [2 * E, E], F32R)
        pick_f = sb("pick_f", [2 * E, E])

        xT = [sb(f"xT{i}", [P, SEQ]) for i in range(3)]
        xh0, xl0 = sb("xh0", [P, SEQ], F32R), sb("xl0", [P, SEQ], F32R)
        xh2, xl2 = sb("xh2", [P, SEQ], F32R), sb("xl2", [P, SEQ], F32R)
        xh, xl = {0: xh0, 2: xh2}, {0: xl0, 2: xl2}
        resid = sb("resid", [P, SEQ])
        x_tok = sb("x_tok", [P, NT, P])
        out_tok = sb("out_tok", [P, NT, P])
        g_r = sb("g_r", [P, CH], at=where["out_tok"])
        stats = sb("stats", [P, NT, 6])
        mv = sb("mv", [P, NT, 2])
        var_eps = sb("var_eps", [P, NT])
        rstd = sb("rstd", [P, NT])
        r8 = [sb(f"r8_{i}", [P, NT, E]) for i in range(6)]
        r1 = [sb(f"r1_{i}", [P, NT]) for i in range(6)]
        wstack = sb("wstack", [P, NT, 2 * E], F32R)
        wT = [sb(f"wT{i}", [2 * E, SEQ], F32R) for i in range(2)]
        mpart = sb("mpart", [P, KV, G, NT, NC])
        mneg = sb("mneg", [P, KV * NC, G * TPC])
        mrow = sb("mrow", [G * TPC, KV * NC, P], F32R)
        h_last = sb("h_last", [P, 1])
        gT = sb("gT", [P, KV, SEQ])
        rden = sb("rden", [P, TPC, G])
        dsum = sb("dsum", [P, CH])
        val = sb("val", [P, NT, KV * HD])
        qk = sb("qk", [P, NT, NH * HD])
        g_a = sb("g_a", [P, CH], at=where["qk"])
        g_z = sb("g_z", [P, CH], at=where["qk"] + 4 * CH)
        g_s = sb("g_s", [P, CH], at=where["qk"] + 8 * CH)
        hid = sb("hid", [P, SEQ], at=where["qk"] + 12 * CH)
        kT = sb("kT", [3 * HD + 1, KV, SEQ], F32R)
        region = where["kT"]
        qT = sb("qT", [3 * HD + 1, KV * NC, G, CH], F32R)
        stack = sb("stack", [P, 2, QT, NH, 3 * HD], F32R)
        rotated = [sb(f"rotated{i}", [P, QT, NH, RH]) for i in range(4)]
        prob = [sb(f"prob{n}", [P, G, CH], at=at)
                for n, at in enumerate((where["stack"], where["stack"] + 4 * G * CH, where["xh2"]))]
        psum = [sb(f"psum{n}", [P, 2, CH], at=where[at]) for n, at in enumerate(("xT2", "wT1"))]
        raw = sb("raw", [P, 5, E * 2 * P], at=region)
        e_t = sb("e_t", [P, CH], at=region)
        e_u = sb("e_u", [P, NU, CH], at=region + 4 * CH)
        e_h = sb("e_h", [P, NB, CH], at=region + 4 * CH * (1 + NU))
        e_hh = sb("e_hh", [P, NX, CH], F32R, at=region + 4 * CH * (1 + NU + NB))
        e_hl = sb("e_hl", [P, NX, CH], F32R, at=region + 4 * CH * (1 + NU + NB + NX))
        assert max(ends) <= nc.sbuf_usable_end, (max(ends), nc.sbuf_usable_end)

        RNN, MAXB, OB, SB0 = 4, 0, 2, 5
        DB = (3,) * (KV * NC - 1) + (7,)
        SPREAD, DOWN = 4, 6
        HEADB = 2

        const_made, vec_const = sem("const_made"), sem("vec_const")
        small_in, raw_in = sem("small_in"), [sem(f"raw_in{n}") for n in range(5)]
        names = [f"norm{i}_{x}" for i in range(4) for x in ("in", "turned", "var", "rstd", "done", "back")]
        names += [f"{x}{i}_made" for i in range(3) for x in ("xh", "xT", "xl")]
        names += [f"route{i}_{x}" for i in range(2) for x in ("mm", "logit", "exp", "weight", "turned", "wT")]
        names += [f"mix{i}_{x}" for i in range(2) for x in ("mm", "act", "h", "hi", "lo", "down")]
        names += """gate_mm gate_made hidden_mm hidden_made gru_state gru_sum vec_step
            hi_made lo_made
            proj_mm proj_read rope_done stack_act stack_vec heads_turned headT_made
            max_mm max_red max_neg mrow_turned mrow_made mrow_placed
            score_mm prob_made pv_mm pv_read pair_summed third_summed fourth_summed den_mm den_read den_turned rden_made
            rden_mm att_made wo_mm out_stored next_in ones_row""".split()
        s = {n: sem(n) for n in names}
        turn_sems = range(s[names[0]].num, s[names[-1]].num + 1)
        assert len(turn_sems) == len(names)

        raws = [("up0", up_w[0]), ("gate_up", gate_up_w), ("down0", down_w[0]),
                ("up1", up_w[1]), ("down1", down_w[1])]

        PAIR_ORDER = (PAIRS - 1,) + tuple(range(PAIRS - 1))

        def headT(pair, q):
            if pair < G * KV // 2:
                g, j = divmod(2 * pair, G)
                c, half = divmod(q, 2)
                return qT[0:3 * HD, c * KV + g, j:j + 2, half * QT * P:(half + 1) * QT * P]
            return kT[0:3 * HD, :, q * QT * P:(q + 1) * QT * P]

        def turn(steps, b=None, nxt=None):
            held = set(x for st in steps for x in (st[0], st[:2]))
            attention, experts0, experts1 = "scores" in held, "mix0" in held, "mix1" in held
            first, final = not attention, not experts0
            x_of = {0: xT[0], 1: xT[1], 2: xT[0 if final else 2]}
            xh_of, xl_of = ({0: a[0], 2: a[0 if final else 2]} for a in (xh, xl))
            wT_of = (wT[0], wT[0 if final else 1])

            def bank(what, c):
                if what in ("gate", "norm0", "back0", "route0"):
                    return 7 if first else RNN
                if what in ("out", "norm2", "back2", "route1"):
                    return (4, 3)[c] if final else 7
                return 3 if what == "back1" and not (first and c == 0) else 7

            def proj_bank(n):
                return 7 if first and n < PROJ_OPS else (3, 7)[n % 2]

            def proj_ordinal(t):
                return t // TPC * PROJ_OPS + t % TPC

            def ordinal(gc):
                return gc - 1 if gc else (KV * NC - 1 if attention else 0)

            def max_ordinal(m):
                return ordinal(m // MU) * MU + m % MU

            max_bank, before = {}, {}
            inverted = {}
            den_before = {}
            last_in, third, dens = {}, None, 0
            for name, *which in steps:
                if name == "stack":
                    third = 6
                elif name == "scores":
                    third = None if which[0] >= NT and 1 <= which[0] % NT <= 3 else 3
                elif name == "denominators":
                    den_before[which[0]], third = last_in.get(DB[which[0]], 0), None
                elif name == "gated":
                    dens += 1
                elif name == "max":
                    m = which[0]
                    max_bank[m] = min((0, 1) if third is None else (0, 1, third), key=lambda x: last_in.get(x, 0))
                    before[m] = last_in.get(max_bank[m], 0)
                    last_in[max_bank[m]] = max_ordinal(m) + 1
                    inverted[m] = dens if max_bank[m] == 3 else 0
            def add_probabilities(engine, part, k):
                gc, t = divmod(k, NT)
                heads, to = {"pair": (slice(0, 2), psum[0][:]), "third": (slice(2, 3), psum[1][:, 0:1]),
                             "fourth": (slice(3, 4), psum[1][:, 1:2])}[part]
                if t == 0:
                    return
                engine.wait_ge(s["prob_made"], G * k + heads.stop)
                if t == 1 and gc >= 1:
                    engine.wait_ge(s["den_mm"], gc)
                if t >= 2:
                    engine.wait_ge(s[f"{part}_summed"], summed(k) - 1)
                engine.tensor_tensor(to, to if t >= 2 else prob[(k - 1) % NP][:, heads],
                                     prob[k % NP][:, heads], ALU.add).then_inc(s[f"{part}_summed"], 1)

            with nc.Block() as block:
                @block.tensor
                def _(pe):
                    def mm3(to, w, k, xhi, xlo, start=True, stop=True):
                        cols = slice(k * P, (k + 1) * P)
                        pe.matmul(to, w[:, 0, cols], xhi, start=start, stop=False)
                        pe.matmul(to, w[:, 1, cols], xhi, start=False, stop=False)
                        return pe.matmul(to, w[:, 0, cols], xlo, start=False, stop=stop)

                    def gate(k):
                        c, layer = divmod(k, 2)
                        if k == 0 and not attention:
                            pe.wait_ge(small_in, SMALL)
                            pe.wait_ge(const_made, 4)
                            pe.wait_ge(vec_const, 3)
                        if k >= 1:
                            pe.wait_ge(s["gru_state"], k)
                        if layer == 0 and c >= 1 and first:
                            pe.wait_ge(s["route0_wT"], c)
                        x = (x_seq if layer == 0 else hid)[:, c * CH:(c + 1) * CH]
                        pe.matmul(ps[:, bank("gate", 0)], gru_w[:, layer, 0:P], x, start=True, stop=True)\
                          .then_inc(s["gate_mm"], 1)

                    def hidden(k):
                        c, layer = divmod(k, 2)
                        pe.wait_ge(s["gate_made"], k + 1)
                        x = (x_seq if layer == 0 else hid)[:, c * CH:(c + 1) * CH]
                        pe.matmul(ps[:, bank("gate", 0)], gru_w[:, layer, P:2 * P], x, start=True, stop=True)\
                          .then_inc(s["hidden_mm"], 1)

                    def norm_turn(i, c):
                        whole = (i == 0 and not first) or (i == 2 and not final)
                        pe.wait_ge(s[f"norm{i}_in"], NC if whole else c + 1)
                        if c >= 1:
                            pe.wait_ge(s[f"norm{i}_done"], c)
                            if i in (0, 2):
                                pe.wait_ge(s[f"xT{i}_made"], c)
                            if i == 1:
                                pe.wait_ge(s["proj_read"], c * PROJ_OPS)
                        elif i == 1 and experts1:
                            pe.wait_ge(s["route1_wT"], NC)
                        elif i == 1:
                            pe.wait_ge(s["route0_wT"], NC)
                        elif i == 3 and "ogate" in held:
                            pe.wait_ge(s["proj_read"], NC * PROJ_OPS)
                        for t in range(TPC):
                            tok = (c * TPC + t) * P
                            mm = pe.transpose(ps[:, bank(f"norm{i}", c), t * P:(t + 1) * P],
                                              resid[:, tok:tok + P], ident[:])
                        mm.then_inc(s[f"norm{i}_turned"], 1)

                    def norm_back(i, c):
                        pe.wait_ge(s[f"norm{i}_done"], c + 1)
                        if c >= 1:
                            pe.wait_ge(s[f"xT{i}_made"], c)
                        for t in range(TPC):
                            mm = pe.transpose(ps[:, bank(f"back{i}", c), t * P:(t + 1) * P],
                                              x_tok[:, c * TPC + t], ident[:])
                        mm.then_inc(s[f"norm{i}_back"], 1)

                    def logits(i, c, n):
                        pe.wait_ge(s[f"xT{2 * i}_made"], c + n)
                        for t in range(c * TPC, (c + n) * TPC):
                            mm = pe.matmul(ps[:, bank(f"route{i}", c), t * E:(t + 1) * E],
                                           x_of[2 * i][:, t * P:(t + 1) * P], route_w[:, i], start=True, stop=True)
                        mm.then_inc(s[f"route{i}_mm"], n)

                    def weights(i, c):
                        pe.wait_ge(s[f"route{i}_weight"], c + 1)
                        if c >= 1:
                            pe.wait_ge(s[f"route{i}_wT"], c)
                        for t in range(TPC):
                            mm = pe.transpose(ps[0:2 * E, bank(f"route{i}", c), t * P:(t + 1) * P],
                                              wstack[:, c * TPC + t].bitcast(F32), ident[:])
                        mm.then_inc(s[f"route{i}_turned"], 1)

                    def spread(i, n):
                        c, eh, tok = unit(n)
                        m = n // HALF
                        if m >= 2:
                            pe.wait_ge(s[f"mix{i}_h"], 2 * (m - 1))
                        pe.matmul(ps[:, SPREAD + m % 2], pick[:, eh // HALF:eh // HALF + 1].broadcast_to([2 * E, P]),
                                  wT_of[i][:, tok], start=True, stop=True)

                    def down(i, n):
                        c, eh, tok = unit(n)
                        if eh == 0 and c >= 1:
                            pe.wait_ge(s[f"norm{1 + 2 * i}_in"], c)
                        if eh == 0 and i == 1:
                            if c == 0 and experts0:
                                pe.wait_ge(s["norm1_in"], NC)
                            pe.matmul(ps[:, DOWN], down_b[:], wT_of[1][:, tok].bitcast(F32), start=True, stop=False)
                        pe.wait_ge(s[f"mix{i}_hi"], n + 1)
                        pe.wait_ge(s[f"mix{i}_lo"], n + 1)
                        mm3(ps[:, DOWN], down_w[i], eh, e_hh[:, n % NX], e_hl[:, n % NX],
                            start=i == 0 and eh == 0, stop=eh == E * HALF - 1).then_inc(s[f"mix{i}_down"], 1)

                    def mix0(n):
                        if n < UNITS and n % (E * HALF) == 0:
                            pe.wait_ge(s["route0_wT"], unit(n)[0] + 1)
                            pe.wait_ge(s["xl0_made"], unit(n)[0] + 1)
                        if n == 0:
                            if not attention:
                                pe.wait_ge(s["lo_made"], len(raws))
                        if n == 1 and attention:
                            pe.wait_ge(s["pv_read"], KV * NC)
                        if n < UNITS:
                            c, eh, tok = unit(n)
                            if n % HALF == 0:
                                spread(0, n)
                            if n >= 2:
                                pe.wait_ge(s["mix0_h"], n - 1)
                            mm3(ps[:, 2 * (n % 2)], up_w[0], eh, xh0[:, tok], xl0[:, tok])
                            mm3(ps[:, 2 * (n % 2) + 1], gate_up_w, eh, xh0[:, tok], xl0[:, tok])\
                                .then_inc(s["mix0_mm"], 1)
                        if n >= LAG:
                            down(0, n - LAG)

                    def mix1(n):
                        if n < UNITS and n % (E * HALF) == 0:
                            pe.wait_ge(s["route1_wT"], unit(n)[0] + 1)
                            pe.wait_ge(s["xl2_made"], unit(n)[0] + 1)
                        if n == 0 and experts0:
                            pe.wait_ge(s["mix0_h"], UNITS)
                        if n == 2 and final:
                            pe.wait_ge(s["pv_read"], KV * NC)
                        if n < UNITS:
                            c, eh, tok = unit(n)
                            if n % HALF == 0:
                                spread(1, n)
                            if n >= 3:
                                pe.wait_ge(s["mix1_act"], n - 2)
                            mm3(ps[:, n % 3], up_w[1], eh, xh_of[2][:, tok], xl_of[2][:, tok]).then_inc(s["mix1_mm"], 1)
                        if n >= LAG:
                            down(1, n - LAG)

                    def qkv(t):
                        n = proj_ordinal(t)
                        if t % TPC == 0:
                            pe.wait_ge(s["xT1_made"], t // TPC + 1)
                        project(n, ps[:, proj_bank(n), 0:QKV], xT[1][:, t * P:(t + 1) * P], qkv_w[:])

                    def project(n, to, lhsT, rhs):
                        if n % PROJ_OPS:
                            pe.wait_ge(s["proj_read"], n if proj_bank(n - 1) == proj_bank(n) else n - 1)
                        pe.matmul(to, lhsT, rhs, start=True, stop=True).then_inc(s["proj_mm"], 1)

                    def ogate(g, c):
                        n = c * PROJ_OPS + TPC + g
                        project(n, ps[:, proj_bank(n)], ogate_w[:, g * P:(g + 1) * P], xT[1][:, c * CH:(c + 1) * CH])

                    def turn_heads(q, turned):
                        n, pair = q * PAIRS + turned, PAIR_ORDER[turned]
                        if turned == 0:
                            pe.wait_ge(s["stack_act"], 2 * (q + 1))
                            pe.wait_ge(s["stack_vec"], q + 1)
                        if n == 0:
                            pe.wait_ge(s["proj_read"], NC * PROJ_OPS)
                        if n >= 4:
                            pe.wait_ge(s["headT_made"], n - 3)
                        for j in range(2):
                            for t in range(QT):
                                mm = pe.transpose(ps[0:3 * HD, HEADB + n % 4, (j * QT + t) * P:(j * QT + t + 1) * P],
                                                  stack[:, q % 2, t, 2 * pair + j].bitcast(F32), ident[:])
                        mm.then_inc(s["heads_turned"], 1)

                    def max_(m):
                        g, j, t, c = max_unit(m)
                        n = max_ordinal(m)
                        if m == 0:
                            pe.wait_ge(s["headT_made"], NQ // NC * PAIRS)
                        if m == MU // NC:
                            pe.wait_ge(s["headT_made"], (NQ - 1) * PAIRS + 1)
                        if before[m]:
                            pe.wait_ge(s["max_red"], before[m])
                        if inverted[m]:
                            pe.wait_ge(s["att_made"], inverted[m])
                        if m % MU == 0 and ordinal(m // MU) >= 1:
                            pe.wait_ge(s["mrow_made"], ordinal(m // MU))
                        pe.matmul(ps[:, max_bank[m]], qT[0:3 * HD, m // MU, j, t % TPC * P:(t % TPC + 1) * P],
                                  kT[0:3 * HD, g, c * CH:(c + 1) * CH], start=True, stop=True)\
                          .then_inc(s["max_mm"], 1)

                    def row(gc):
                        pe.wait_ge(s["max_neg"], ordinal(gc) + 1)
                        pe.transpose(ps[0:G * TPC, MAXB, 0:P], mneg[:, gc], ident[:]).then_inc(s["mrow_turned"], 1)

                    def scores(k, p):
                        gc, t = divmod(k, NT)
                        if t == 0 and p == 0 and gc >= 1:
                            pe.wait_ge(s["mrow_placed"], 16 * (ordinal(gc) + 1))
                        for j in (2 * p, 2 * p + 1):
                            n = k * G + j
                            if n >= 3:
                                pe.wait_ge(s["prob_made"], n - 2)
                            pe.matmul(ps[:, SB0 + n % 3], kT[:, group_and_chunk(gc)[0], t * P:(t + 1) * P], qT[:, gc, j],
                                      start=True, stop=True).then_inc(s["score_mm"], 1)

                    def values(k):
                        gc, t = divmod(k, NT)
                        g = group_and_chunk(gc)[0]
                        pe.wait_ge(s["prob_made"], G * (k + 1))
                        if t == 0 and gc >= 1:
                            pe.wait_ge(s["pv_read"], gc)
                        for j in range(G):
                            mm = pe.matmul(ps[j * HD:(j + 1) * HD, OB], val[:, t, g * HD:(g + 1) * HD],
                                           prob[k % NP][:, j], start=t == 0, stop=t == NT - 1)
                        mm.then_inc(s["pv_mm"], 1)

                    def denominators(gc):
                        for x in ("pair", "third", "fourth"):
                            pe.wait_ge(s[f"{x}_summed"], (NT - 1) * (gc + 1))
                        if gc >= 1:
                            pe.wait_ge(s["att_made"], gc)
                        if den_before[gc]:
                            pe.wait_ge(s["max_red"], den_before[gc])
                        for j in range(G):
                            mm = pe.matmul(ps[j * HD:(j + 1) * HD, DB[gc]], ones[:], psum[j // 2][:, j % 2],
                                           start=True, stop=True)
                        mm.then_inc(s["den_mm"], 1)

                    def invert(gc):
                        pe.wait_ge(s["den_read"], gc + 1)
                        for t in range(TPC):
                            mm = pe.transpose(ps[:, DB[gc], t * P:(t + 1) * P], dsum[:, t * P:(t + 1) * P], ident[:])
                        mm.then_inc(s["den_turned"], 1)

                    def gated(gc):
                        pe.wait_ge(s["rden_made"], gc + 1)
                        for t in range(TPC):
                            for j in range(G):
                                mm = pe.matmul(ps[j * HD:(j + 1) * HD, DB[gc], t * P:(t + 1) * P],
                                               rden[:, t, j:j + 1].broadcast_to([P, HD]), ident[:], start=True, stop=True)
                        mm.then_inc(s["rden_mm"], 1)

                    def project_out(c):
                        pe.wait_ge(s["att_made"], KV * (c + 1) if final else KV * NC)
                        if c >= 1:
                            pe.wait_ge(s["norm2_in"], c)
                        for g in range(KV):
                            mm = pe.matmul(ps[:, bank("out", c)], out_w[:, g], gT[:, g, c * CH:(c + 1) * CH],
                                           start=g == 0, stop=g == KV - 1)
                        mm.then_inc(s["wo_mm"], 1)

                    own = dict(gate=gate, hidden=hidden, norm_turn=norm_turn, norm_back=norm_back, logits=logits,
                               weights=weights, mix0=mix0, mix1=mix1, qkv=qkv, ogate=ogate, turn_heads=turn_heads,
                               max=max_, row=row, scores=scores, values=values, denominators=denominators,
                               invert=invert, gated=gated, project_out=project_out)
                    for name, *which in steps:
                        if name in own:
                            own[name](*which)

                @block.scalar
                def _(act):
                    def split(n):
                        act.wait_ge(raw_in[n], 16)
                        act.activation(raws[n][1][:, 0], raw[:, n], ACT.Copy).then_inc(s["hi_made"], 1)

                    def gate(k):
                        layer = k % 2
                        act.wait_ge(s["gate_mm"], k + 1)
                        act.activation(g_z[:], ps[:, bank("gate", 0)], ACT.Tanh, scale=0.5, bias=gru_hb[:, layer, 0:1])\
                           .then_inc(s["gate_made"], 1)

                    def hidden(k):
                        layer = k % 2
                        act.wait_ge(s["hidden_mm"], k + 1)
                        act.activation(g_s[:], ps[:, bank("gate", 0)], ACT.Tanh, scale=0.5, bias=gru_hb[:, layer, 1:2])\
                           .then_inc(s["hidden_made"], 1)

                    def norm_back(i, c):
                        tok = slice(c * CH, (c + 1) * CH)
                        act.wait_ge(s[f"norm{i}_back"], c + 1)
                        if i != 1:
                            act.activation(xh_of[i][:, tok], ps[:, bank(f"back{i}", c)], ACT.Copy).then_inc(s[f"xh{i}_made"], 1)
                        act.activation(x_of[i][:, tok], ps[:, bank(f"back{i}", c)], ACT.Copy).then_inc(s[f"xT{i}_made"], 1)

                    def choose(i, c, n, part):
                        if part == 0:
                            ts = slice(c * TPC, (c + n) * TPC)
                            act.wait_ge(s[f"route{i}_logit"], c + n)
                            act.activation(r8[1][:, ts], r8[0][:, ts], ACT.Exp).then_inc(s[f"route{i}_exp"], n)

                    def weights(i, c):
                        act.wait_ge(s[f"route{i}_turned"], c + 1)
                        act.activation(wT_of[i][:, c * CH:(c + 1) * CH], ps[0:2 * E, bank(f"route{i}", c)], ACT.Copy)\
                           .then_inc(s[f"route{i}_wT"], 1)

                    def hi(i, n):
                        act.wait_ge(s[f"mix{i}_h"], n + 1)
                        if n >= NX:
                            act.wait_ge(s[f"mix{i}_down"], n - NX + 1)
                        act.activation(e_hh[:, n % NX], e_h[:, n % NB], ACT.Copy).then_inc(s[f"mix{i}_hi"], 1)

                    def mix0(n):
                        if n < UNITS:
                            act.wait_ge(s["mix0_mm"], n + 1)
                            if n >= NU:
                                act.wait_ge(s["mix0_h"], n - NU + 1)
                            act.activation(e_u[:, n % NU], ps[:, 2 * (n % 2)], ACT.Silu).then_inc(s["mix0_act"], 1)
                        if 1 <= n <= UNITS:
                            hi(0, n - 1)

                    def mix1(n):
                        if n == 0 and experts0:
                            act.wait_ge(s["mix0_down"], UNITS)
                        if n < UNITS:
                            eh = n % (E * HALF)
                            act.wait_ge(s["mix1_mm"], n + 1)
                            if n >= NU:
                                act.wait_ge(s["mix1_h"], n - NU + 1)
                            act.activation(e_u[:, n % NU], ps[:, n % 3], ACT.Relu, bias=up_b[:, eh:eh + 1])\
                               .then_inc(s["mix1_act"], 1)
                        if 1 <= n <= UNITS:
                            hi(1, n - 1)

                    def qkv(t):
                        n = proj_ordinal(t)
                        act.wait_ge(s["proj_mm"], n + 1)
                        act.activation(qk[:, t], ps[:, proj_bank(n), 0:NH * HD], ACT.Copy)
                        act.activation(val[:, t], ps[:, proj_bank(n), NH * HD:QKV], ACT.Copy)\
                           .then_inc(s["proj_read"], 1)

                    def ogate(g, c):
                        n = c * PROJ_OPS + TPC + g
                        act.wait_ge(s["proj_mm"], n + 1)
                        act.activation(gT[:, g, c * CH:(c + 1) * CH], ps[:, proj_bank(n)], ACT.Silu)\
                           .then_inc(s["proj_read"], 1)

                    def stack_(q):
                        if q == 0:
                            act.wait_ge(s["mix1_down" if experts1 else "mix0_down"], UNITS)
                        act.wait_ge(s["rope_done"], q + 1)
                        if q >= 2:
                            act.wait_ge(s["heads_turned"], PAIRS * (q - 1))
                        x = qk[:, q * QT:(q + 1) * QT].rearrange("p t (h f) -> p t h f", f=HD)
                        act.activation(stack[:, q % 2, :, :, 0:HD], x, ACT.Copy).then_inc(s["stack_act"], 1)
                        act.activation(stack[:, q % 2, :, 0:HEADS, 2 * HD:3 * HD], x[:, :, 0:HEADS], ACT.Copy)
                        act.activation(stack[:, q % 2, :, HEADS:NH, HD:2 * HD], x[:, :, HEADS:NH], ACT.Copy)\
                           .then_inc(s["stack_act"], 1)

                    def turn_heads(q, turned):
                        n = q * PAIRS + turned
                        act.wait_ge(s["heads_turned"], n + 1)
                        got = ps[0:3 * HD, HEADB + n % 4].rearrange("p (j t) -> p j t", j=2)
                        act.activation(headT(PAIR_ORDER[turned], q), got, ACT.Copy).then_inc(s["headT_made"], 1)

                    def scores(k, p):
                        for j in (2 * p, 2 * p + 1):
                            act.wait_ge(s["score_mm"], k * G + j + 1)
                            if k >= NP:
                                act.wait_ge(s["pv_mm"], k - NP + 1)
                                act.wait_ge(s[("pair_summed", "pair_summed", "third_summed", "fourth_summed")[j]],
                                            summed(k - NP) + ((k - NP) % NT == 0))
                            act.activation(prob[k % NP][:, j], ps[:, SB0 + (k * G + j) % 3], ACT.Exp, scale=SCALE)\
                               .then_inc(s["prob_made"], 1)

                    def denominators(gc):
                        act.wait_ge(s["den_mm"], gc + 1)
                        if gc >= 1:
                            act.wait_ge(s["den_turned"], gc)
                        act.activation(dsum[:], ps[:, DB[gc]], ACT.Copy).then_inc(s["den_read"], 1)

                    own = dict(split=split, gate=gate, hidden=hidden, norm_back=norm_back, choose=choose,
                               weights=weights, mix0=mix0, mix1=mix1, qkv=qkv, ogate=ogate, stack=stack_,
                               turn_heads=turn_heads, scores=scores, denominators=denominators)
                    for name, *which in steps:
                        if name in own:
                            own[name](*which)

                @block.vector
                def _(vec):
                    chain = [0]

                    def marked(ins):
                        chain[0] += 1
                        ins.then_inc(s["vec_step"], 1)

                    def last_marked():
                        vec.wait_ge(s["vec_step"], chain[0])

                    def then(ins):
                        marked(ins)
                        last_marked()

                    def split(n):
                        vec.wait_ge(s["hi_made"], n + 1)
                        w = raws[n][1]
                        vec.tensor_tensor(w[:, 1], raw[:, n], w[:, 0].bitcast(F32), ALU.subtract)\
                           .then_inc(s["lo_made"], 1)

                    def state(k, part):
                        c, layer = divmod(k, 2)
                        to = (hid if layer == 0 else resid)[:, c * CH:(c + 1) * CH]
                        if part == 0:
                            vec.wait_ge(s["gate_made"], k + 1)
                            vec.tensor_scalar(g_a[:], g_z[:], -0.5, 0.5, ALU.mult, ALU.add)
                            vec.wait_ge(s["hidden_made"], k + 1)
                            vec.tensor_scalar(g_r[:], ps[:, bank("gate", 0)], gru_b[:, layer, 1:2], 0.0, ALU.add, ALU.max)
                            marked(vec.tensor_scalar(g_s[:], g_s[:], 0.0, 0.5, ALU.min, ALU.mult))
                        elif part == 1:
                            last_marked()
                            marked(vec.scalar_tensor_tensor(g_s[:], g_s[:], 0.5, g_r[:], ALU.add, ALU.add))
                        elif part == 2:
                            last_marked()
                            marked(vec.scalar_tensor_tensor(g_z[:], g_z[:], 1.0, g_s[:], ALU.add, ALU.mult))
                        elif part == 3:
                            last_marked()
                            first = 1.0 if c == 0 else hid[:, c * CH - 1:c * CH] if layer == 0 else h_last[:]
                            vec.tensor_tensor_scan(to, g_a[:], g_z[:], first, ALU.mult, ALU.add)\
                               .then_inc(s["gru_state"], 1)
                        else:
                            vec.wait_ge(s["gru_state"], k + 1)
                            if c == 0:
                                then(vec.tensor_copy(h_last[:], to[:, CH - 1:CH]))
                            vec.scalar_tensor_tensor(to, to, 0.5, x_seq[:, c * CH:(c + 1) * CH], ALU.mult, ALU.add)\
                               .then_inc(s["norm0_in"], 1)

                    def norm_turn(i, c):
                        vec.wait_ge(s[f"norm{i}_turned"], c + 1)
                        tile = [ps[:, bank(f"norm{i}", c), t * P:(t + 1) * P] for t in range(TPC)]
                        ts = range(TPC * c, TPC * (c + 1))
                        cs = slice(TPC * c, TPC * (c + 1))
                        for t in ts:
                            last = vec.bn_stats(stats[:, t], tile[t % TPC])
                        then(last)
                        for t in ts:
                            last = vec.bn_aggr(mv[:, t], stats[:, t])
                        then(last)
                        vec.tensor_scalar(var_eps[:, cs], mv[:, cs, 1], EPS, None, ALU.add)\
                           .then_inc(s[f"norm{i}_var"], 1)

                    def norm_apply(i, c):
                        vec.wait_ge(s[f"norm{i}_rstd"], c + 1)
                        tile = [ps[:, bank(f"norm{i}", c), t * P:(t + 1) * P] for t in range(TPC)]
                        to = out_tok if i == 3 else x_tok
                        for t in range(TPC * c, TPC * (c + 1)):
                            last = vec.tensor_scalar(to[:, t], tile[t % TPC], mv[:, t, 0:1], rstd[:, t:t + 1],
                                                     ALU.subtract, ALU.mult)
                        last.then_inc(s[f"norm{i}_done"], 1)

                    def norm_back(i, c):
                        if i == 1:
                            return
                        tok = slice(c * CH, (c + 1) * CH)
                        vec.wait_ge(s[f"xT{i}_made"], c + 1)
                        vec.tensor_tensor(xl_of[i][:, tok], x_of[i][:, tok], xh_of[i][:, tok].bitcast(F32), ALU.subtract)\
                           .then_inc(s[f"xl{i}_made"], 1)

                    def over(x, n):
                        return x.rearrange("p (t e) -> p t e", e=1).broadcast_to([P, n * TPC, E])

                    def logits(i, c, n):
                        ts = slice(c * TPC, (c + n) * TPC)
                        lg, pr, mx = r8[0][:, ts], r8[2][:, ts], r1[0][:, ts]
                        vec.wait_ge(s[f"route{i}_mm"], c + n)
                        got = ps[:, bank(f"route{i}", c), c * TPC * E:(c + n) * TPC * E].rearrange("p (t e) -> p t e", e=E)
                        if i == 0:
                            then(vec.tensor_copy(pr, got))
                        else:
                            bias = route_b[:].rearrange("p (t e) -> p t e", t=1).broadcast_to([P, n * TPC, E])
                            then(vec.tensor_tensor(pr, got, bias, ALU.add))
                        then(vec.tensor_reduce(mx, pr, AX.X, ALU.max))
                        vec.tensor_tensor(lg, pr, over(mx, n), ALU.subtract).then_inc(s[f"route{i}_logit"], n)

                    def choose(i, c, n, part):
                        ts = slice(c * TPC, (c + n) * TPC)
                        ex, pr, eq, oh1, oh2 = (r[:, ts] for r in r8[1:])
                        sm, m1, v, m2, tmp = (r[:, ts] for r in r1[1:])
                        ranks = rank[:].rearrange("p (t e) -> p t e", t=1).broadcast_to([P, n * TPC, E])

                        def first_of(x, m, oh):
                            then(vec.tensor_reduce(m, x, AX.X, ALU.max))
                            then(vec.tensor_tensor(eq, x, over(m, n), ALU.is_equal))
                            then(vec.tensor_tensor(eq, eq, ranks, ALU.mult))
                            then(vec.tensor_reduce(v, eq, AX.X, ALU.max))
                            marked(vec.tensor_tensor(oh, eq, over(v, n), ALU.is_equal))

                        if part == 0:
                            vec.wait_ge(s[f"route{i}_exp"], c + n)
                            then(vec.tensor_reduce(sm, ex, AX.X, ALU.add))
                            then(vec.reciprocal(tmp, sm))
                            marked(vec.tensor_tensor(pr, ex, over(tmp, n), ALU.mult))
                            return
                        last_marked()
                        if part == 1:
                            first_of(pr, m1, oh1)
                        elif part == 2:
                            then(vec.scalar_tensor_tensor(ex, oh1, -2.0, pr, ALU.mult, ALU.add))
                            first_of(ex, m2, oh2)
                        elif part == 3:
                            then(vec.tensor_tensor(oh1, oh1, oh2, ALU.add))
                            marked(vec.tensor_tensor(pr, pr, oh1, ALU.mult))
                            if i == 0:
                                last_marked()
                                then(vec.tensor_tensor(sm, m1, m2, ALU.add))
                                then(vec.reciprocal(tmp, sm))
                                marked(vec.tensor_tensor(pr, pr, over(tmp, n), ALU.mult))
                        else:
                            if i == 1 and ("logits", 0) in held:
                                vec.wait_ge(s["route0_turned"], c + n)
                            then(vec.tensor_copy(wstack[:, ts, 0:E], pr))
                            vec.tensor_tensor(wstack[:, ts, E:2 * E], pr, wstack[:, ts, 0:E].bitcast(F32),
                                              ALU.subtract).then_inc(s[f"route{i}_weight"], n)

                    def add_down(i, n):
                        c, eh, tok = unit(n)
                        if eh == E * HALF - 1:
                            if i == 0 and ("norm_turn", 2) in held:
                                vec.wait_ge(s["norm2_turned"], c + 1)
                            if i == 1 and ("norm_turn", 1) in held:
                                vec.wait_ge(s["norm1_turned"], c + 1)
                            vec.wait_ge(s[f"mix{i}_down"], n + 1)
                            vec.tensor_tensor(resid[:, tok], x_of[2 * i][:, tok], ps[:, DOWN], ALU.add)\
                               .then_inc(s[f"norm{1 + 2 * i}_in"], 1)

                    def mix0(n):
                        if n < UNITS:
                            vec.wait_ge(s["mix0_act"], n + 1)
                            then(vec.tensor_tensor(e_t[:], e_u[:, n % NU], ps[:, SPREAD + n // HALF % 2], ALU.mult))
                            if n >= NB:
                                vec.wait_ge(s["mix0_lo"], n - NB + 1)
                            vec.tensor_tensor(e_h[:, n % NB], e_t[:], ps[:, 2 * (n % 2) + 1], ALU.mult)\
                               .then_inc(s["mix0_h"], 1)
                            vec.wait_ge(s["mix0_h"], n + 1)
                        if n >= LAG:
                            add_down(0, n - LAG)

                    def mix1(n):
                        if n == 0 and experts0:
                            vec.wait_ge(s["mix0_lo"], UNITS)
                        if n < UNITS:
                            vec.wait_ge(s["mix1_act"], n + 1)
                            if n >= NB:
                                vec.wait_ge(s["mix1_lo"], n - NB + 1)
                            vec.tensor_tensor(e_h[:, n % NB], e_u[:, n % NU], ps[:, SPREAD + n // HALF % 2], ALU.mult)\
                               .then_inc(s["mix1_h"], 1)
                        if n >= LAG:
                            add_down(1, n - LAG)

                    def rope(q):
                        cs = slice(q * QT, (q + 1) * QT)
                        vec.wait_ge(s["proj_read"], proj_ordinal(QT * (q + 1) - 1) + 1)
                        if q >= 1:
                            vec.wait_ge(s["rope_done"], q)
                        x = qk[:, cs].rearrange("p t (h f) -> p t h f", f=HD)
                        x1, x2 = x[:, :, :, 0:RH], x[:, :, :, RH:ROT]
                        co, si = (w[:, cs].rearrange("p t (h f) -> p t h f", h=1)
                                  .broadcast_to([P, QT, NH, RH]) for w in (cos, sin))
                        x1c, x2s, x2c, x1s = (r[:] for r in rotated)
                        vec.tensor_tensor(x1c, x1, co, ALU.mult)
                        vec.tensor_tensor(x2s, x2, si, ALU.mult)
                        vec.tensor_tensor(x2c, x2, co, ALU.mult)
                        then(vec.tensor_tensor(x1s, x1, si, ALU.mult))
                        vec.tensor_tensor(x1, x1c, x2s, ALU.subtract)
                        vec.tensor_tensor(x2, x2c, x1s, ALU.add).then_inc(s["rope_done"], 1)

                    def stack_(q):
                        if q == 0:
                            vec.wait_ge(s["mix1_down" if experts1 else "mix0_down"], UNITS)
                        if q >= 2:
                            vec.wait_ge(s["heads_turned"], PAIRS * (q - 1))
                        x = qk[:, q * QT:(q + 1) * QT].rearrange("p t (h f) -> p t h f", f=HD)
                        vec.wait_ge(s["rope_done"], q + 1)
                        vec.wait_ge(s["stack_act"], 2 * q + 1)
                        to = stack[:, q % 2]
                        qs, ks = slice(0, HEADS), slice(HEADS, NH)
                        hi = to[:, :, :, 0:HD].bitcast(F32)
                        vec.tensor_tensor(to[:, :, qs, HD:2 * HD], x[:, :, qs], hi[:, :, qs], ALU.subtract)
                        vec.tensor_tensor(to[:, :, ks, 2 * HD:3 * HD], x[:, :, ks], hi[:, :, ks], ALU.subtract)\
                           .then_inc(s["stack_vec"], 1)

                    def max_(m):
                        g, j, t, c = max_unit(m)
                        vec.wait_ge(s["max_mm"], max_ordinal(m) + 1)
                        vec.tensor_reduce(mpart[:, g, j, t, c:c + 1], ps[:, max_bank[m]], AX.X, ALU.max)\
                           .then_inc(s["max_red"], 1)

                    def row(gc):
                        n = ordinal(gc)
                        g, c = group_and_chunk(gc)
                        vec.wait_ge(s["max_red"], (n + 1) * MU)
                        vec.tensor_reduce(mneg[:, gc].rearrange("p (j t) -> p j t", j=G),
                                          mpart[:, g, :, c * TPC:(c + 1) * TPC],
                                          AX.X, ALU.max, negate=True).then_inc(s["max_neg"], 1)
                        vec.wait_ge(s["mrow_turned"], n + 1)
                        vec.tensor_copy(mrow[:, gc], ps[0:G * TPC, MAXB, 0:P]).then_inc(s["mrow_made"], 1)

                    def sum_(k):
                        for part in ("third", "fourth") if k // NT == KV * NC - 1 else ("fourth",):
                            add_probabilities(vec, part, k)

                    def take_out(gc):
                        g, c = group_and_chunk(gc)
                        to = gT[:, g, c * CH:(c + 1) * CH]
                        vec.wait_ge(s["pv_mm"], NT * (gc + 1))
                        vec.tensor_tensor(to, to, ps[:, OB], ALU.mult).then_inc(s["pv_read"], 1)

                    def invert(gc):
                        vec.wait_ge(s["den_turned"], gc + 1)
                        one_of_head = ps[:, DB[gc]].rearrange("p (t j f) -> p t j f", t=TPC, j=G)[:, :, :, 0]
                        vec.reciprocal(rden[:], one_of_head).then_inc(s["rden_made"], 1)

                    def gated(gc):
                        g, c = group_and_chunk(gc)
                        to = gT[:, g, c * CH:(c + 1) * CH]
                        vec.wait_ge(s["rden_mm"], gc + 1)
                        vec.wait_ge(s["pv_read"], gc + 1)
                        vec.tensor_tensor(to, to, ps[:, DB[gc]], ALU.mult).then_inc(s["att_made"], 1)

                    def project_out(c):
                        tok = slice(c * CH, (c + 1) * CH)
                        vec.wait_ge(s["wo_mm"], c + 1)
                        vec.tensor_tensor(resid[:, tok], xT[1][:, tok], ps[:, bank("out", c)], ALU.add)\
                           .then_inc(s["norm2_in"], 1)

                    own = dict(split=split, state=state, norm_turn=norm_turn, norm_apply=norm_apply,
                               norm_back=norm_back, logits=logits, choose=choose, mix0=mix0, mix1=mix1, rope=rope, stack=stack_,
                               max=max_, row=row, sum=sum_, take_out=take_out, invert=invert,
                               gated=gated, project_out=project_out)
                    for name, *which in steps:
                        if name in own:
                            own[name](*which)

                @block.gpsimd
                def _(pool):
                    def norm_turn(i, c):
                        cs = slice(TPC * c, TPC * (c + 1))
                        pool.wait_ge(s[f"norm{i}_var"], c + 1)
                        pool.tensor_tensor(rstd[:, cs], var_eps[:, cs], minus_half[:], ALU.pow)\
                            .then_inc(s[f"norm{i}_rstd"], 1)

                    def sum_(k):
                        for part in ("pair",) if k // NT == KV * NC - 1 else ("pair", "third"):
                            add_probabilities(pool, part, k)

                    def lo(i, n):
                        pool.wait_ge(s[f"mix{i}_hi"], n + 1)
                        if n >= NX:
                            pool.wait_ge(s[f"mix{i}_down"], n - NX + 1)
                        pool.tensor_tensor(e_hl[:, n % NX], e_h[:, n % NB], e_hh[:, n % NX].bitcast(F32),
                                           ALU.subtract).then_inc(s[f"mix{i}_lo"], 1)

                    def mix0(n):
                        if 1 <= n <= UNITS:
                            lo(0, n - 1)

                    def mix1(n):
                        if n == 1 and experts0:
                            pool.wait_ge(s["mix0_down"], UNITS)
                        if 1 <= n <= UNITS:
                            lo(1, n - 1)

                    def stack_(q):
                        if q == 0:
                            pool.wait_ge(s["mix1_down" if experts1 else "mix0_down"], UNITS)
                            pool.wait_ge(s["norm1_rstd"], NC)
                            pool.memset(kT[3 * HD:3 * HD + 1].bitcast(F32), 1.0).then_inc(s["ones_row"], 1)
                            pool.wait_ge(s["ones_row"], 1)

                    own = dict(norm_turn=norm_turn, mix0=mix0, mix1=mix1, stack=stack_, sum=sum_)
                    for name, *which in steps:
                        if name in own:
                            own[name](*which)

                @block.sync
                def _(sp):
                    def next_x():
                        sp.wait_ge(s["norm0_in"], NC)
                        sp.dma_start(x_seq[:], d["xT"][nxt]).then_inc(s["next_in"], 16)

                    def row(gc):
                        sp.wait_ge(s["mrow_made"], ordinal(gc) + 1)
                        sp.dma_start(qT[3 * HD:3 * HD + 1, gc].bitcast(F32), mrow[:, gc].bitcast(F32))\
                          .then_inc(s["mrow_placed"], 16)

                    def store(c):
                        sp.wait_ge(s["norm3_done"], c + 1)
                        sp.dma_start(out[b, c], out_tok[:, c * TPC:(c + 1) * TPC]).then_inc(s["out_stored"], 16)

                    own = dict(next_x=next_x, row=row, store=store)
                    for name, *which in steps:
                        if name in own:
                            own[name](*which)
                    rows = sum(st[0] == "row" for st in steps)
                    sp.wait_ge(s["mrow_placed"], 16 * rows)
                    if ("store", 0) in steps:
                        sp.wait_ge(s["out_stored"], 16 * NC)
                    if ("next_x",) in steps:
                        sp.wait_ge(s["next_in"], 16)

        def clear():
            with nc.Block() as block:
                @block.sync
                def _(sp):
                    sp.sem_clear(turn_sems)

        small = [(x_seq[:], d["xT"][0]), (gru_w[:], d["gru_w"]), (gru_b[:], d["gru_b"]), (route_w[:], d["route_w"]),
                 (route_b[:], d["route_b"]), (up_b[:], d["up_b"]), (down_b[:], d["down_b"]),
                 (qkv_w[:], d["qkv_w"]), (ogate_w[:], d["ogate_w"]), (out_w[:], d["out_w"]),
                 (cos[:], d["cos"]), (sin[:], d["sin"])]
        SMALL = 16 * len(small)

        with nc.Block() as block:
            @block.sync
            def _(sp):
                for to, of in small:
                    sp.dma_start(to, of).then_inc(small_in, 16)
                for n in range(0, len(raws)):
                    sp.dma_start(raw[:, n], d[raws[n][0]]).then_inc(raw_in[n], 16)

            @block.vector
            def _(vec):
                vec.memset(ones[:], 1.0)
                vec.memset(minus_half[:], -0.5)
                for e in range(E):
                    last = vec.memset(rank[:, e:e + 1], float(E - e))
                last.then_inc(vec_const, 1)
                vec.wait_ge(const_made, 4)
                vec.tensor_copy(pick[:], pick_f[:]).then_inc(vec_const, 1)
                vec.wait_ge(small_in, SMALL)
                vec.tensor_scalar(gru_hb[:], gru_b[:], 0.5, None, ALU.mult)
                vec.tensor_scalar(gru_w[:, 1], gru_w[:, 1], 0.5, None, ALU.mult).then_inc(vec_const, 1)

            @block.gpsimd
            def _(pool):
                pool.memset(ident[:], 0.0).then_inc(const_made, 1)
                pool.memset(pick_f[:], 0.0).then_inc(const_made, 1)
                pool.wait_ge(const_made, 2)
                pool.affine_select(out=ident[:], in_=ident[:], compare_op=ALU.not_equal, fill=1.0,
                                   base=0, pattern=[[-1, P]], channel_multiplier=1)
                pool.affine_select(out=pick_f[:], in_=pick_f[:], compare_op=ALU.not_equal, fill=1.0,
                                   base=0, pattern=[[-1, E]], channel_multiplier=1).then_inc(const_made, 1)
                pool.wait_ge(const_made, 3)
                pool.affine_select(out=pick_f[:], in_=pick_f[:], compare_op=ALU.not_equal, fill=1.0,
                                   base=-E, pattern=[[-1, E]], channel_multiplier=1).then_inc(const_made, 1)

        G0, G1 = (recurrence_steps(c) for c in range(NC))
        P0, P1 = (project_steps(c) for c in range(NC))
        entry = [norm_steps(0, c) + route_steps(0, c) for c in range(NC)]
        join = [[("project_out", c)] + norm_steps(2, c) + route_steps(1, c) for c in range(NC)]
        experts, half = first_expert_steps(), UNITS // NC
        splits = [("split", n) for n in range(len(raws))]
        turn(woven(G0 + entry[0], splits, 0, 3)
             + woven(experts[:half], G1 + entry[1], 0, 1)
             + woven(experts[half:], P0, LAG, 1)
             + P1 + head_steps(), nxt=1)
        clear()
        beside_c = woven(attention_steps(), G0 + G1 + norm_steps(0, 0) + norm_steps(0, 1)
                         + route_steps(0, 0, NC), 20, 7)
        beside_d = woven(experts, last_part_steps() + [("project_out", c) for c in range(NC)]
                         + norm_steps(2, 0) + norm_steps(2, 1) + route_steps(1, 0, NC), 1, 2)
        beside_e = woven(second_expert_steps(), P0 + P1, 1, 2)
        beside_h = woven(head_steps(), last_norm_steps(), 3, 2)
        with nc.Fori(0, BATCH - 1) as b:
            turn(beside_c + beside_d + beside_e + beside_h, b=b, nxt=(b + 2) % BATCH)
            clear()
        steps = attention_steps()
        through = steps.index(("gated", KV - 1)) + 1
        turn(woven(steps, join[0], through, 5) + woven(second_expert_steps(), last_part_steps() + join[1], 0, 1)
             + last_norm_steps(), b=BATCH - 1)


def rotary_table():
    inv = (1.0 / np.float32(10000.0) ** (np.arange(0, ROT, 2, dtype=np.float32) / np.float32(ROT)))
    freqs = np.arange(SEQ, dtype=np.float32)[:, None] * inv.astype(np.float32)[None, :]
    split = lambda a: np.ascontiguousarray(a.astype(np.float32).reshape(NT, P, RH).transpose(1, 0, 2))
    return split(np.cos(freqs)), split(np.sin(freqs))


def lay_out(a):
    t = np.ascontiguousarray
    cos, sin = rotary_table()
    by_partition = lambda w: t(w.reshape(-1, HALF, P, P).transpose(2, 0, 1, 3).reshape(P, -1))
    wq, wk, wv = a["L1_attn_Wq"], a["L1_attn_Wk"], a["L1_attn_Wv"]
    return {
        "xT": t(a["L0_attn_x"].transpose(0, 2, 1)),
        "gru_w": t(np.stack([a["L0_attn_W0"].T, a["L0_attn_W1"].T], 1)),
        "gru_b": t(np.stack([a["L0_attn_b0"].reshape(2, P).T, a["L0_attn_b1"].reshape(2, P).T], 1)),
        "route_w": t(np.stack([a["L0_ffn_wg"].T, a["L1_ffn_gate_w"].T], 1)),
        "route_b": t(np.repeat(a["L1_ffn_gate_b"][None], P, 0)),
        "up0": t(a["L0_ffn_w1"].transpose(2, 0, 1).reshape(P, -1)),
        "gate_up": t(a["L0_ffn_w3"].transpose(2, 0, 1).reshape(P, -1)),
        "down0": by_partition(a["L0_ffn_w2"].transpose(0, 2, 1)),
        "up1": t(a["L1_ffn_w1"].transpose(1, 0, 2).reshape(P, -1)),
        "down1": by_partition(a["L1_ffn_w2"]),
        "up_b": t(a["L1_ffn_b1"].reshape(E * HALF, P).T),
        "down_b": t(np.concatenate([a["L1_ffn_b2"]] * 2, 0)),
        "qkv_w": t(np.concatenate([wq[:, :HEADS * HD], wk, wv], 1)),
        "ogate_w": t(wq[:, HEADS * HD:]),
        "out_w": t(a["L1_attn_Wo"].reshape(KV, P, P).transpose(1, 0, 2)),
        "cos": cos,
        "sin": sin,
    }


def kernel(**inputs):
    import concourse.bacc as _bacc
    from concourse.bass_utils import run_bass_kernel_spmd as _run

    arrays = lay_out({k: np.asarray(v) for k, v in inputs.items()})
    nc = _bacc.Bacc("TRN2", target_bir_lowering=False, num_devices=1, dynamic_dma_scratch_size=1024)
    ins = {k: nc.dram_tensor(f"in_{k}", v.shape, mybir.dt.from_np(v.dtype), kind="ExternalInput").ap()
           for k, v in arrays.items()}
    out = nc.dram_tensor("out", (BATCH, SEQ, P), F32, kind="ExternalOutput").ap()
    build_network(nc, ins, out.rearrange("b (c t p) f -> b c p t f", c=NC, t=TPC))
    r = _run(nc, [{f"in_{k}": v for k, v in arrays.items()}], core_ids=[0])
    return r.results[0]["out"]
```
